# Optimizing a Trainium2 kernel written in Bass

```python
import numpy as np
import jax
import jax.numpy as jnp

def _softmax(x, axis=-1):
    return jax.nn.softmax(x, axis=axis)

def _gelu(x):
    return jax.nn.gelu(x, approximate=True)

def _silu(x):
    return jax.nn.silu(x)

def _sigmoid(x):
    return jax.nn.sigmoid(x)

def _layernorm(x, axis=-1, eps=1e-05):
    m = jnp.mean(x, axis=axis, keepdims=True)
    v = jnp.var(x, axis=axis, keepdims=True)
    return (x - m) / jnp.sqrt(v + eps)

def _scatter_add(tgt, idx, src, axis=0):
    return tgt.at[idx].add(src)

def _segment_sum(src, seg, n):
    return jax.ops.segment_sum(src, seg, n)
kernel_name = 'mk_gnn_ffn_d1_gnn_r32_1a6ee2'

def setup_inputs(seed: int=0):
    np.random.seed(seed)
    _w = jnp.asarray

    def _rec_inputs():
        import jax
        import jax.numpy as jnp
        _gk = jax.random.key(seed)
        x = -7.329e-05 + 0.9999 * jax.random.normal(jax.random.fold_in(_gk, 1), (10000, 512), jnp.float32)
        src = jax.random.randint(jax.random.fold_in(_gk, 2), (5000,), 0, 10000, jnp.int32)
        dst = jnp.minimum((10000 * jax.random.uniform(jax.random.fold_in(_gk, 3), (5000,)) ** 2.0).astype(jnp.int32), 9999)
        _o = jnp.argsort(dst, stable=True)
        src = src[_o]
        dst = dst[_o]
        edge_weight = jax.random.uniform(jax.random.fold_in(_gk, 12), (5000,), jnp.float32, 0.0, 0.999999)
        return (x, src, dst, edge_weight)
    x, src, dst, edge_weight = _rec_inputs()

    def _L0_gnn_setup():
        import jax, jax.numpy as jnp
        import numpy as np
        N = 3125
        D_IN = 512
        D_OUT = 512
        E = 100000
        key = jax.random.key(seed)
        ks = jax.random.split(key, 10)
        stdv = 1.0 / np.sqrt(D_OUT)
        return {'x': jax.random.normal(ks[0], (N, D_IN), dtype=jnp.float32), 'w1': jax.random.uniform(ks[1], (D_IN, D_OUT), jnp.float32, -stdv, stdv), 'w2': jax.random.uniform(ks[2], (D_IN, D_OUT), jnp.float32, -stdv, stdv), 'w3': jax.random.uniform(ks[3], (D_IN, D_OUT), jnp.float32, -stdv, stdv), 'b1': jax.random.uniform(ks[4], (D_OUT,), jnp.float32, -stdv, stdv), 'b2': jax.random.uniform(ks[5], (D_OUT,), jnp.float32, -stdv, stdv), 'b3': jax.random.uniform(ks[6], (D_OUT,), jnp.float32, -stdv, stdv), 'edge_row': jax.random.randint(ks[7], (E,), 0, N, dtype=jnp.int32), 'edge_col': jax.random.randint(ks[8], (E,), 0, N, dtype=jnp.int32), 'edge_val': jax.random.uniform(ks[9], (E,), dtype=jnp.float32)}
    _L0_gnn_all = _L0_gnn_setup()
    _L0_gnn_in = {k: v for k, v in _L0_gnn_all.items() if k in ('w1', 'w2', 'w3', 'b1', 'b2', 'b3')}
    del _L0_gnn_all

    def _L0_ffn_setup():
        import jax, jax.numpy as jnp
        import numpy as np
        B, S, D, F, E, K = (4, 64, 512, 64, 8, 2)
        key = jax.random.key(seed)
        kx, kg, kw, kv, k2 = jax.random.split(key, 5)
        scale = 0.02
        return {'x': jax.random.normal(kx, (B, S, D), dtype=jnp.float32), 'Wg': jax.random.normal(kg, (D, E), dtype=jnp.float32) * scale, 'W': jax.random.normal(kw, (E, D, F), dtype=jnp.float32) * scale, 'V': jax.random.normal(kv, (E, D, F), dtype=jnp.float32) * scale, 'W2': jax.random.normal(k2, (E, F, D), dtype=jnp.float32) * scale}
    _L0_ffn_all = _L0_ffn_setup()
    _L0_ffn_in = {k: v for k, v in _L0_ffn_all.items() if k in ('Wg', 'W', 'V', 'W2')}
    del _L0_ffn_all
    return {'x': x, 'src': src, 'dst': dst, 'edge_weight': edge_weight, 'L0_gnn_w1': _L0_gnn_in['w1'], 'L0_gnn_w2': _L0_gnn_in['w2'], 'L0_gnn_w3': _L0_gnn_in['w3'], 'L0_gnn_b1': _L0_gnn_in['b1'], 'L0_gnn_b2': _L0_gnn_in['b2'], 'L0_gnn_b3': _L0_gnn_in['b3'], 'L0_ffn_Wg': _L0_ffn_in['Wg'], 'L0_ffn_W': _L0_ffn_in['W'], 'L0_ffn_V': _L0_ffn_in['V'], 'L0_ffn_W2': _L0_ffn_in['W2']}

def reference(x, src, dst, edge_weight, L0_gnn_w1, L0_gnn_w2, L0_gnn_w3, L0_gnn_b1, L0_gnn_b2, L0_gnn_b3, L0_ffn_Wg, L0_ffn_W, L0_ffn_V, L0_ffn_W2):
    import jax
    import jax.numpy as jnp

    def _L0_gnn_ref(x, w1, w2, w3, b1, b2, b3, edge_row, edge_col, edge_val):
        import jax, jax.numpy as jnp
        import numpy as np
        N = 3125
        D_IN = 512
        D_OUT = 512
        E = 100000
        n = x.shape[0]
        support = x @ w1
        trans = x @ w2 + b2
        gate = jax.nn.sigmoid(x @ w3 + b3)
        msgs = support[edge_col] * edge_val[:, None]
        agg = jax.ops.segment_sum(msgs, edge_row, num_segments=n)
        out = jax.nn.relu(agg + b1)
        return trans + gate * (out - trans)

    def _L0_ffn_ref(x, Wg, W, V, W2):
        import jax, jax.numpy as jnp
        import numpy as np
        B, S, D, F, E, K = (4, 64, 512, 64, 8, 2)
        gate_logits = jnp.einsum('bsd,de->bse', x, Wg)
        topv, topi = jax.lax.top_k(gate_logits, K)
        w = jax.nn.softmax(topv, axis=-1)
        gw = jnp.sum(w[..., None] * jax.nn.one_hot(topi, E, dtype=x.dtype), axis=-2)
        y = jnp.zeros_like(x)
        n_experts = W.shape[0]
        for e in range(n_experts):
            h = jax.nn.silu(jnp.einsum('bsd,df->bsf', x, W[e])) * jnp.einsum('bsd,df->bsf', x, V[e])
            y = y + gw[..., e:e + 1] * jnp.einsum('bsf,fd->bsd', h, W2[e])
        return y
    x = x + _L0_gnn_ref(_layernorm(x, axis=-1), L0_gnn_w1, L0_gnn_w2, L0_gnn_w3, L0_gnn_b1, L0_gnn_b2, L0_gnn_b3, src, dst, edge_weight)
    x = x + _L0_ffn_ref(_layernorm(x, axis=-1)[None], L0_ffn_Wg, L0_ffn_W, L0_ffn_V, L0_ffn_W2)[0]
    return x

_drawn_inputs = setup_inputs


def setup_inputs(seed=0):
    import zlib

    import numpy as np

    out = dict(_drawn_inputs(seed))
    spreads = {}
    factors = {'L0_gnn_b1': 7.491,
     'L0_gnn_b2': 4.388,
     'L0_gnn_b3': 8.0,
     'L0_ffn_Wg': 5.496,
     'L0_ffn_W': 4.862,
     'L0_ffn_V': 4.745,
     'L0_ffn_W2': 4.753}
    for name, (base, spread) in spreads.items():
        noise = np.random.default_rng([zlib.crc32(name.encode()), seed]).standard_normal(out[name].shape)
        drawn = base * np.exp(spread * noise) if base else spread * noise
        out[name] = jnp.asarray(drawn.astype(out[name].dtype))
    for name, factor in factors.items():
        out[name] = (out[name] * factor).astype(out[name].dtype)
    return out
```

```python
from contextlib import ExitStack

import concourse.bass as bass
from concourse import mybir

F32 = mybir.dt.float32
F32R = mybir.dt.float32r
I32 = mybir.dt.int32
U32 = mybir.dt.uint32
ALU = mybir.AluOpType
ACT = mybir.ActivationFunctionType

P = 128
LEAD = 9
EPS = 1e-5
EDGE_SLOTS = 4


class At:

    def __init__(self, turn, place, unroll):
        self.turn, self.place, self.unroll = turn, place, unroll
        self.n = turn * unroll + place

    def plus(self, k):
        turns, place = divmod(self.place + k, self.unroll)
        return At(self.turn + turns, place, self.unroll)

    def within(self, count):
        return not isinstance(self.n, int) or 0 <= self.n < count


def pair(n):
    return At(n // 2, n % 2, 2)


def four(n):
    return At(n // EDGE_SLOTS, n % EDGE_SLOTS, EDGE_SLOTS)


def after(eng, sem, count):
    if not isinstance(count, int) or count > 0:
        eng.wait_ge(sem, count)


def after_apart(eng, *waits):
    if isinstance(waits[0][1], int):
        for sem, count in waits:
            after(eng, sem, count)
        return
    counts = [eng.snap(count) for _, count in waits]
    for count in counts:
        eng.compute_val(count)
    eng.wait_ge(waits[0][0], 1)
    for (sem, _), count in zip(waits, counts):
        eng.wait_ge(sem, count)


def gnn_experts_kernel(nc, x, src_rows, src_cols, dst_cols, val_cols, w1, w2, w3, b1, b2, b3,
                       wg, wW, wV, wO, out):
    ROWS, D = x.shape
    TILES = ROWS // P
    C = D // P
    EDGE_TILES = src_cols.shape[1]
    NE = wg.shape[1]
    FE = D // NE
    SPARE = ROWS
    X_RING = LEAD + 4
    FILL_ROWS = 512
    FILLS = (ROWS + P) // FILL_ROWS
    assert D == 512 and ROWS % P == 0 and (TILES - LEAD) % 2 == 0 and LEAD % 2 == 1
    assert EDGE_TILES % EDGE_SLOTS == 0 and (ROWS + P) % FILL_ROWS == 0 and FILLS >= 2 * LEAD

    agg = nc.dram_tensor("agg", (ROWS + P, D), F32, kind="Internal").ap()

    with ExitStack() as ctx:
        def sb(name, shape, dt=F32):
            return ctx.enter_context(nc.sbuf_tensor(name, shape, dt))

        def sem(name):
            return ctx.enter_context(nc.semaphore(name))

        ident = sb("ident", [P, P])
        before = sb("before", [P, P])
        minus_half = sb("minus_half", [P, 1])
        expert_i = sb("expert_i", [P, NE], I32)
        expert_f = sb("expert_f", [P, NE])
        spare_i = sb("spare_i", [P, 1], I32)
        spare_f = sb("spare_f", [P, 1])
        b2_all = sb("b2_all", [P, D])
        b3_all = sb("b3_all", [P, D])

        stage = [sb(f"stage{i}", [P, C, D]) for i in range(2)]
        def parts(name, n=D):
            return sb(name + "_hi", [P, C, n], F32R), sb(name + "_lo", [P, C, n], F32R)
        w1O = parts("w1_then_wO")
        w2p, w3p, wWp, wVp = parts("w2"), parts("w3"), parts("wW"), parts("wV")
        wgp = parts("wg", NE)
        wg_raw = sb("wg_raw", [P, C, NE])
        weights = [(w3, w3p), (w2, w2p), (w1, w1O), (wW, wWp), (wV, wVp), (wO, w1O)]
        W3, W2, W1, WW, WV, WO = range(len(weights))

        x_ring = sb("x_ring", [P, X_RING, D])
        t_ring = sb("t_ring", [P, LEAD, D])
        g_ring = sb("g_ring", [P, LEAD, D])
        xn = sb("xn", [P, D])
        xnT = [(sb(f"xnT_hi{i}", [P, C, P], F32R), sb(f"xnT_lo{i}", [P, C, P], F32R)) for i in range(2)]
        a_st = sb("a_st", [P, 6])
        a_mv = sb("a_mv", [P, 2])
        a_rs = sb("a_rs", [P, 1])

        work = sb("work", [P, 10, D])
        edge_x = [work[:, i, :] for i in range(4)]
        edge_xn = work[:, 4, :]
        edge_msg = [work[:, 5 + i, :] for i in range(4)]
        b1_all = work[:, 9, :]
        agg_in = [work[:, i, :] for i in range(2)]
        diff, mixed, x1n, z_tanh, act, h = (work[:, 2 + i, :] for i in range(6))
        out_sb = [work[:, 8 + i, :] for i in range(2)]

        workr = [sb(f"workr{i}", [P, D], F32R) for i in range(4)]
        edge_hi, edge_lo = workr[0], workr[1]
        def chunked(a):
            return a[:, :].rearrange("p (c m) -> p c m", c=C)
        x1nT = (chunked(workr[0]), chunked(workr[1]))
        hT = (chunked(workr[2]), chunked(workr[3]))
        sumT = xnT

        same = sb("same", [P, P], F32R)
        same_before = sb("same_before", [P, P])
        src_row = [sb(f"src_row{i}", [P, P], I32) for i in range(4)]
        src_i = sb("src_i", [P, EDGE_TILES], I32)
        dst_i = sb("dst_i", [P, EDGE_TILES], I32)
        val = sb("val", [P, EDGE_TILES])
        src_f = sb("src_f", [P, EDGE_TILES])
        to_spare = sb("to_spare", [P, EDGE_TILES])
        target = sb("target", [P, EDGE_TILES], I32)
        dst_idx = [sb(f"dst_idx{i}", [P, 1], I32) for i in range(4)]
        src_idx = [sb(f"src_idx{i}", [P, 1], I32) for i in range(2)]
        earlier = sb("earlier", [P, 1])
        shift = sb("shift", [P, 1])
        e_st = sb("e_st", [P, 6])
        e_mv = [sb(f"e_mv{i}", [P, 2]) for i in range(2)]
        e_rs = [sb(f"e_rs{i}", [P, 1]) for i in range(2)]
        e_rv = [sb(f"e_rv{i}", [P, 1]) for i in range(2)]

        b_st = sb("b_st", [P, 6])
        b_mv = sb("b_mv", [P, 2])
        b_rs = sb("b_rs", [P, 1])
        logit = sb("logit", [P, NE])
        best = sb("best", [P, 8])
        best_i = sb("best_i", [P, 8], U32)
        best_f = sb("best_f", [P, 2])
        gap = sb("gap", [P, 1])
        e2 = sb("e2", [P, 1])
        total = sb("total", [P, 1])
        share = sb("share", [P, 2])
        gw1 = sb("gw1", [P, NE])
        gw2 = sb("gw2", [P, NE])
        gw = sb("gw", [P, NE])

        bank = [ctx.enter_context(nc.psum_tensor(f"bank{i}", [P, D], F32)) for i in range(8)]
        p_xnT_hT, p_x1nT, p_gate, p_trans, p_zw, p_zv, p_y, p_logit = bank
        p_sumT = [p_zw, p_zv]
        p_msg = [p_y, p_logit]

        consts_ld = sem("consts_ld")
        edges_ld = sem("edges_ld")
        b1_ld = sem("b1_ld")
        filled = sem("filled")
        stage_ld = [sem(f"stage_ld{i}") for i in range(2)]
        wg_ld = sem("wg_ld")
        w_hi = sem("w_hi")
        w_lo = sem("w_lo")
        wg_hi = sem("wg_hi")
        wg_lo = sem("wg_lo")
        memset_done = sem("memset_done")
        ident_rdy = sem("ident_rdy")
        before_rdy = sem("before_rdy")
        iota_rdy = sem("iota_rdy")
        spare_rdy = sem("spare_rdy")
        expert_rdy = sem("expert_rdy")
        src_f_rdy = sem("src_f_rdy")
        to_spare_rdy = sem("to_spare_rdy")

        x_ld = [sem(f"x_ld{i}") for i in range(2)]
        a_stats = sem("a_stats")
        a_moments = sem("a_moments")
        a_var = sem("a_var")
        a_rstd = sem("a_rstd")
        xn_rdy = sem("xn_rdy")
        xnT_ps = sem("xnT_ps")
        xnT_hi = sem("xnT_hi")
        xnT_lo = sem("xnT_lo")
        gate_ps = sem("gate_ps")
        trans_ps = sem("trans_ps")
        gate_sb = sem("gate_sb")
        gate_tanh = sem("gate_tanh")
        trans_sb = sem("trans_sb")

        src_row_ld = [sem(f"src_row_ld{i}") for i in range(4)]
        dst_idx_rdy = sem("dst_idx_rdy")
        gathered = [sem(f"gathered{i}") for i in range(4)]
        same_rdy = sem("same_rdy")
        earlier_rdy = sem("earlier_rdy")
        shift_rdy = sem("shift_rdy")
        target_rdy = sem("target_rdy")
        e_stats = sem("e_stats")
        e_moments = sem("e_moments")
        e_var = sem("e_var")
        e_rstd = sem("e_rstd")
        e_scale = sem("e_scale")
        edge_xn_rdy = sem("edge_xn_rdy")
        edge_hi_rdy = sem("edge_hi_rdy")
        edge_lo_rdy = sem("edge_lo_rdy")
        sumT_ps = sem("sumT_ps")
        sumT_hi = sem("sumT_hi")
        sumT_lo = sem("sumT_lo")
        msg_ps = sem("msg_ps")
        msg_sb = sem("msg_sb")
        src_idx_rdy = sem("src_idx_rdy")
        added = sem("added")

        agg_ld = [sem(f"agg_ld{i}") for i in range(2)]
        diff_rdy = sem("diff_rdy")
        gated_rdy = sem("gated_rdy")
        mixed_rdy = sem("mixed_rdy")
        x1_rdy = sem("x1_rdy")
        b_stats = sem("b_stats")
        b_moments = sem("b_moments")
        b_var = sem("b_var")
        b_rstd = sem("b_rstd")
        x1n_rdy = sem("x1n_rdy")
        x1nT_ps = sem("x1nT_ps")
        x1nT_hi = sem("x1nT_hi")
        x1nT_lo = sem("x1nT_lo")
        zw_ps = sem("zw_ps")
        zv_ps = sem("zv_ps")
        z_tanh_rdy = sem("z_tanh_rdy")
        silu_rdy = sem("silu_rdy")
        act_rdy = sem("act_rdy")
        logit_rdy = sem("logit_rdy")
        best_rdy = sem("best_rdy")
        best_i_rdy = sem("best_i_rdy")
        gap_rdy = sem("gap_rdy")
        best_f_rdy = sem("best_f_rdy")
        e2_rdy = sem("e2_rdy")
        total_rdy = sem("total_rdy")
        share1_rdy = sem("share1_rdy")
        share2_rdy = sem("share2_rdy")
        gw12_rdy = sem("gw12_rdy")
        gw_rdy = sem("gw_rdy")
        h_rdy = sem("h_rdy")
        hT_ps = sem("hT_ps")
        hT_hi = sem("hT_hi")
        hT_lo = sem("hT_lo")
        y_ps = sem("y_ps")
        out_rdy = sem("out_rdy")
        out_st = [sem(f"out_st{i}") for i in range(2)]

        block = ctx.enter_context(nc.Block())

        @block.sync
        def _(sp):
            def load_weight(i):
                after(sp, w_lo, i - 1)
                sp.dma_start(stage[i % 2][:, :, :],
                             weights[i][0].rearrange("(c p) n -> p c n", p=P)).then_inc(stage_ld[i % 2], 16)

            def load_x(t):
                sp.dma_start(x_ring[:, t.n % X_RING, :], x[bass.ds(t.n * P, P), :]).then_inc(x_ld[t.place], 16)

            def fill(i):
                sp.dma_start(agg[i * FILL_ROWS:(i + 1) * FILL_ROWS, :].rearrange("(a p) d -> p a d", p=P),
                             b1_all.unsqueeze(1).to_broadcast([P, FILL_ROWS // P, D])).then_inc(filled, 16)

            def load_agg(u):
                sp.dma_start(agg_in[u.place], agg[bass.ds(u.n * P, P), :]).then_inc(agg_ld[u.place], 16)

            load_x(pair(0))
            load_weight(W3)
            load_x(pair(1))
            sp.dma_start(b1_all, b1.partition_broadcast(P)).then_inc(b1_ld, 16)
            load_weight(W2)
            sp.dma_start(b3_all[:, :], b3.partition_broadcast(P)).then_inc(consts_ld, 16)
            sp.dma_start(b2_all[:, :], b2.partition_broadcast(P)).then_inc(consts_ld, 16)
            for edge_in, at in ((src_i, src_cols), (dst_i, dst_cols), (val, val_cols)):
                sp.dma_start(edge_in[:, :], at).then_inc(edges_ld, 16)
            sp.wait_ge(b1_ld, 16)
            for t in range(LEAD):
                after(sp, a_stats, t + 1)
                load_x(pair(t + 2))
                for i in range(2 * t, 2 * t + 2):
                    fill(i)
                if t == 1:
                    load_weight(W1)
                if t == 3:
                    load_weight(WW)
            for i in range(2 * LEAD, FILLS):
                fill(i)
            sp.dma_start(wg_raw[:, :, :], wg.rearrange("(c p) n -> p c n", p=P)).then_inc(wg_ld, 16)
            load_weight(WV)

            def load_src_row(k):
                after(sp, same_rdy, k.n - EDGE_SLOTS + 1)
                sp.dma_start(src_row[k.place][:, :],
                             src_rows[bass.ds(k.n * P, P)].partition_broadcast(P)).then_inc(src_row_ld[k.place], 16)

            for k in range(EDGE_SLOTS):
                load_src_row(four(k))
            with sp.Fori(1, EDGE_TILES // EDGE_SLOTS) as q:
                for place in range(EDGE_SLOTS):
                    load_src_row(At(q, place, EDGE_SLOTS))
            load_weight(WO)

            sp.wait_ge(added, 16 * EDGE_TILES)
            load_agg(pair(0))
            load_agg(pair(1))
            sp.wait_ge(mixed_rdy, 1)
            load_agg(pair(2))

            def rows(u):
                t = u.plus(LEAD)
                if u.plus(3).within(TILES):
                    after(sp, mixed_rdy, u.n + 2)
                    load_agg(u.plus(3))
                if t.plus(2).within(TILES):
                    after_apart(sp, (a_stats, t.n + 1), (out_rdy, u.n - 1))
                    load_x(t.plus(2))
                if u.plus(-1).within(TILES):
                    store_out(u.plus(-1))

            def store_out(v):
                after(sp, out_rdy, v.n + 1)
                sp.dma_start(out[bass.ds(v.n * P, P), :], out_sb[v.place]).then_inc(out_st[v.place], 16)

            rows(pair(0))
            rows(pair(1))
            with sp.Fori(1, (TILES - LEAD) // 2 - 1) as i:
                rows(At(i, 0, 2))
                rows(At(i, 1, 2))
            for u in range(TILES - LEAD - 2, TILES):
                rows(pair(u))
            store_out(pair(TILES - 1))
            for place in range(2):
                sp.wait_ge(out_st[place], 16 * ((TILES + 1 - place) // 2))

        @block.gpsimd
        def _(pool):
            nc.gpsimd.memset(ident[:, :], 0.0).then_inc(memset_done, 1)
            nc.gpsimd.memset(before[:, :], 1.0).then_inc(memset_done, 1)
            nc.gpsimd.iota(expert_i[:, :], pattern=[[1, NE]], base=0, channel_multiplier=0).then_inc(iota_rdy, 1)
            nc.gpsimd.iota(spare_i[:, :], pattern=[[1, 1]], base=SPARE, channel_multiplier=1).then_inc(iota_rdy, 1)
            nc.gpsimd.memset(minus_half[:, :], -0.5).then_inc(memset_done, 1)
            pool.wait_ge(memset_done, 3)
            nc.gpsimd.affine_select(out=ident[:, :], in_=ident[:, :], compare_op=ALU.not_equal, fill=1.0,
                                    base=0, pattern=[[-1, P]], channel_multiplier=1).then_inc(ident_rdy, 1)
            nc.gpsimd.affine_select(out=before[:, :], in_=before[:, :], compare_op=ALU.is_gt, fill=0.0,
                                    base=0, pattern=[[-1, P]], channel_multiplier=1).then_inc(before_rdy, 1)

            def rstd(mv, rs, moments, n, var_rdy, done):
                after_apart(pool, (moments, n + 1))
                nc.gpsimd.tensor_scalar(rs[:, :], mv[:, 1:2], EPS, None, ALU.add).then_inc(var_rdy, 1)
                after(pool, var_rdy, n + 1)
                nc.gpsimd.tensor_tensor(rs[:, :], rs[:, :], minus_half[:, :], ALU.pow).then_inc(done, 1)

            def gather(k):
                nc.gpsimd.tensor_copy(dst_idx[k.place][:, :], dst_i[:, bass.ds(k.n, 1)]).then_inc(dst_idx_rdy, 1)
                after_apart(pool, (dst_idx_rdy, k.n + 1), (edge_xn_rdy, k.n - EDGE_SLOTS + 1))
                pool.indirect_dma_start(
                    out=edge_x[k.place], out_offset=None, in_=x,
                    in_offset=bass.IndirectOffsetOnAxis(ap=dst_idx[k.place][:, 0:1], axis=0),
                ).then_inc(gathered[k.place], 16)

            pool.wait_ge(edges_ld, 48)
            for k in range(EDGE_SLOTS):
                gather(four(k))

            rstd(a_mv, a_rs, a_moments, 0, a_var, a_rstd)
            with pool.Fori(0, LEAD) as t:
                rstd(a_mv, a_rs, a_moments, t + 1, a_var, a_rstd)

            def edge_rstd(k):
                p = k.place % 2
                rstd(e_mv[p], e_rs[p], e_moments, k.n, e_var, e_rstd)
                after(pool, e_rstd, k.n + 1)
                nc.gpsimd.tensor_tensor(e_rv[p][:, :], e_rs[p][:, :], val[:, bass.ds(k.n, 1)],
                                        ALU.mult).then_inc(e_scale, 1)

            def edges(k):
                if k.plus(4).within(EDGE_TILES):
                    gather(k.plus(4))
                if k.plus(3).within(EDGE_TILES):
                    edge_rstd(k.plus(3))
                p = k.place % 2
                after_apart(pool, (target_rdy, k.n + 1))
                nc.gpsimd.tensor_copy(src_idx[p][:, :], target[:, bass.ds(k.n, 1)]).then_inc(src_idx_rdy, 1)
                after_apart(pool, (src_idx_rdy, k.n + 1), (msg_sb, k.n + 1), (added, k.n * 16))
                pool.indirect_dma_start(
                    out=agg, out_offset=bass.IndirectOffsetOnAxis(ap=src_idx[p][:, 0:1], axis=0),
                    in_=edge_msg[k.place], in_offset=None, bounds_check=ROWS + P - 1, compute_op=ALU.add,
                ).then_inc(added, 16)

            for k in range(3):
                edge_rstd(four(k))
            pool.wait_ge(filled, 16 * FILLS)
            for k in range(EDGE_SLOTS):
                edges(four(k))
            with pool.Fori(1, EDGE_TILES // EDGE_SLOTS - 1) as q:
                for place in range(EDGE_SLOTS):
                    edges(At(q, place, EDGE_SLOTS))
            for k in range(EDGE_TILES - EDGE_SLOTS, EDGE_TILES):
                edges(four(k))

            def x1(u):
                after(pool, mixed_rdy, u.n + 1)
                ring = x_ring[:, u.n % X_RING, :]
                nc.gpsimd.tensor_tensor(ring, mixed, ring, ALU.add).then_inc(x1_rdy, 1)

            def rows(u):
                t = u.plus(LEAD)
                after(pool, hT_ps, u.n)
                after(pool, act_rdy, u.n + 1)
                after(pool, gw_rdy, u.n + 1)
                nc.gpsimd.tensor_tensor(
                    h.rearrange("p (e f) -> p e f", e=NE), act.rearrange("p (e f) -> p e f", e=NE),
                    gw[:, :].unsqueeze(2).to_broadcast([P, NE, FE]), ALU.mult).then_inc(h_rdy, 1)
                if u.plus(2).within(TILES):
                    x1(u.plus(2))
                if t.plus(1).within(TILES):
                    rstd(a_mv, a_rs, a_moments, t.n + 1, a_var, a_rstd)
                if u.plus(2).within(TILES):
                    rstd(b_mv, b_rs, b_moments, u.n + 2, b_var, b_rstd)

            for u in range(2):
                x1(pair(u))
                rstd(b_mv, b_rs, b_moments, u, b_var, b_rstd)
            rows(pair(0))
            rows(pair(1))
            with pool.Fori(1, (TILES - LEAD) // 2 - 1) as i:
                rows(At(i, 0, 2))
                rows(At(i, 1, 2))
            for u in range(TILES - LEAD - 2, TILES):
                rows(pair(u))

        @block.scalar
        def _(act_e):
            def weight_hi(i):
                act_e.wait_ge(stage_ld[i % 2], 16 * (i // 2 + 1))
                nc.scalar.activation(weights[i][1][0][:, :, :], stage[i % 2][:, :, :], ACT.Copy).then_inc(w_hi, 1)

            def xnT_high(t):
                after(act_e, trans_ps, t.n - 1)
                after(act_e, xnT_ps, t.n + 1)
                nc.scalar.activation(xnT[t.place][0][:, :, :], chunked(p_xnT_hT), ACT.Copy).then_inc(xnT_hi, 1)

            def gate_act(t):
                after(act_e, gate_sb, t.n + 1)
                ring = g_ring[:, t.n % LEAD, :]
                nc.scalar.activation(ring, ring, ACT.Tanh, scale=0.5).then_inc(gate_tanh, 1)

            weight_hi(W3)
            xnT_high(pair(0))
            weight_hi(W2)

            def ahead(t):
                xnT_high(t.plus(1))
                gate_act(t)

            ahead(pair(0))
            ahead(pair(1))
            with act_e.Fori(1, LEAD // 2) as i:
                ahead(At(i, 0, 2))
                ahead(At(i, 1, 2))
            gate_act(pair(LEAD - 1))

            def edge_high(k):
                after(act_e, edge_xn_rdy, k.n + 1)
                after(act_e, sumT_ps, k.n)
                nc.scalar.activation(edge_hi[:, :], edge_xn, ACT.Copy).then_inc(edge_hi_rdy, 1)

            def sumT_high(k):
                after(act_e, sumT_ps, k.n + 1)
                after(act_e, msg_ps, k.n - 1)
                nc.scalar.activation(sumT[k.place % 2][0][:, :, :], chunked(p_sumT[k.place % 2]),
                                     ACT.Copy).then_inc(sumT_hi, 1)

            def message(k):
                after(act_e, added, (k.n - EDGE_SLOTS + 1) * 16)
                after(act_e, msg_ps, k.n + 1)
                nc.scalar.activation(edge_msg[k.place], p_msg[k.place % 2][:, :], ACT.Copy).then_inc(msg_sb, 1)

            def edges(k):
                if k.plus(1).within(EDGE_TILES):
                    sumT_high(k.plus(1))
                if k.plus(2).within(EDGE_TILES):
                    edge_high(k.plus(2))
                if k.within(EDGE_TILES):
                    message(k)

            weight_hi(W1)
            for k in range(-2, EDGE_SLOTS):
                edges(four(k))
            with act_e.Fori(1, EDGE_TILES // EDGE_SLOTS - 1) as q:
                for place in range(EDGE_SLOTS):
                    edges(At(q, place, EDGE_SLOTS))
            for k in range(EDGE_TILES - EDGE_SLOTS, EDGE_TILES):
                edges(four(k))

            weight_hi(WW)
            weight_hi(WV)
            act_e.wait_ge(wg_ld, 16)
            nc.scalar.activation(wgp[0][:, :, :], wg_raw[:, :, :], ACT.Copy).then_inc(wg_hi, 1)
            weight_hi(WO)

            def x1nT_high(u):
                after(act_e, x1nT_ps, u.n + 1)
                nc.scalar.activation(x1nT[0], chunked(p_x1nT), ACT.Copy).then_inc(x1nT_hi, 1)

            def hT_high(v):
                after(act_e, hT_ps, v.n + 1)
                nc.scalar.activation(hT[0], chunked(p_xnT_hT), ACT.Copy).then_inc(hT_hi, 1)

            def rows(u):
                t = u.plus(LEAD)
                if u.plus(-1).within(TILES):
                    hT_high(u.plus(-1))
                after(act_e, silu_rdy, u.n)
                after(act_e, zw_ps, u.n + 1)
                nc.scalar.activation(z_tanh, p_zw[:, :], ACT.Tanh, scale=0.5).then_inc(z_tanh_rdy, 1)
                if t.within(TILES):
                    xnT_high(t)
                if u.plus(1).within(TILES):
                    x1nT_high(u.plus(1))
                after(act_e, gap_rdy, u.n + 1)
                nc.scalar.activation(e2[:, :], gap[:, :], ACT.Exp).then_inc(e2_rdy, 1)
                if t.within(TILES):
                    gate_act(t)

            x1nT_high(pair(0))
            rows(pair(0))
            rows(pair(1))
            with act_e.Fori(1, (TILES - LEAD) // 2 - 1) as i:
                rows(At(i, 0, 2))
                rows(At(i, 1, 2))
            for u in range(TILES - LEAD - 2, TILES):
                rows(pair(u))
            hT_high(pair(TILES - 1))

        @block.vector
        def _(dve):
            def f32(a):
                return a.bitcast(F32)

            def low_part(out, whole, high, have_high, count, done):
                after(dve, have_high, count)
                nc.vector.tensor_tensor(out, whole, f32(high), ALU.subtract).then_inc(done, 1)

            def weight_lo(i):
                hi, lo = weights[i][1]
                low_part(lo[:, :, :], stage[i % 2][:, :, :], hi[:, :, :], w_hi, i + 1, w_lo)

            def a_moments_of(t):
                after(dve, x_ld[t.place], 16 * (t.turn + 1))
                nc.vector.bn_stats(a_st[:, :], x_ring[:, t.n % X_RING, :]).then_inc(a_stats, 1)
                after_apart(dve, (a_stats, t.n + 1))
                nc.vector.bn_aggr(a_mv[:, :], a_st[:, :]).then_inc(a_moments, 1)

            def a_norm(t):
                after(dve, a_rstd, t.n + 1)
                nc.vector.tensor_scalar(xn[:, :], x_ring[:, t.n % X_RING, :], a_mv[:, 0:1], a_rs[:, :],
                                        ALU.subtract, ALU.mult).then_inc(xn_rdy, 1)

            def xnT_low(t):
                hi, lo = xnT[t.place]
                low_part(lo[:, :, :], chunked(p_xnT_hT), hi[:, :, :], xnT_hi, t.n + 1, xnT_lo)

            def gate_bias(t):
                after(dve, gate_ps, t.n + 1)
                nc.vector.tensor_tensor(g_ring[:, t.n % LEAD, :], p_gate[:, :], b3_all[:, :],
                                        ALU.add).then_inc(gate_sb, 1)

            def trans_bias(t):
                after(dve, trans_ps, t.n + 1)
                nc.vector.tensor_tensor(t_ring[:, t.n % LEAD, :], p_trans[:, :], b2_all[:, :],
                                        ALU.add).then_inc(trans_sb, 1)

            a_moments_of(pair(0))
            a_norm(pair(0))
            weight_lo(W3)
            xnT_low(pair(0))
            weight_lo(W2)
            dve.wait_ge(consts_ld, 32)

            def ahead(t):
                a_moments_of(t.plus(1))
                a_norm(t.plus(1))
                gate_bias(t)
                if not (isinstance(t.n, int) and t.n == LEAD - 1):
                    xnT_low(t.plus(1))
                trans_bias(t)

            with dve.Fori(0, LEAD // 2) as i:
                ahead(At(i, 0, 2))
                ahead(At(i, 1, 2))
            ahead(pair(LEAD - 1))

            dve.wait_ge(iota_rdy, 2)
            nc.vector.tensor_copy(spare_f[:, :], spare_i[:, :]).then_inc(spare_rdy, 1)
            nc.vector.tensor_copy(expert_f[:, :], expert_i[:, :]).then_inc(expert_rdy, 1)
            dve.wait_ge(edges_ld, 48)
            nc.vector.tensor_copy(src_f[:, :], src_i[:, :]).then_inc(src_f_rdy, 1)
            dve.wait_ge(spare_rdy, 1)
            dve.wait_ge(src_f_rdy, 1)
            nc.vector.tensor_scalar(to_spare[:, :], src_f[:, :], -1.0, spare_f[:, :],
                                    ALU.mult, ALU.add).then_inc(to_spare_rdy, 1)
            dve.wait_ge(to_spare_rdy, 1)
            dve.wait_ge(before_rdy, 1)
            weight_lo(W1)

            def e_moments_of(k):
                p = k.place % 2
                after(dve, gathered[k.place], 16 * (k.turn + 1))
                nc.vector.bn_stats(e_st[:, :], edge_x[k.place]).then_inc(e_stats, 1)
                after_apart(dve, (e_stats, k.n + 1))
                nc.vector.bn_aggr(e_mv[p][:, :], e_st[:, :]).then_inc(e_moments, 1)

            def same_target(k):
                after(dve, sumT_ps, k.n)
                after(dve, src_row_ld[k.place], 16 * (k.turn + 1))
                nc.vector.tensor_scalar(same[:, :], src_row[k.place][:, :], src_f[:, bass.ds(k.n, 1)], None,
                                        ALU.is_equal).then_inc(same_rdy, 1)
                after(dve, same_rdy, k.n + 1)
                nc.vector.tensor_tensor_reduce(out=same_before[:, :], in0=f32(same[:, :]), in1=before[:, :],
                                               scale=1.0, scalar=0.0, op0=ALU.mult, op1=ALU.add,
                                               accum_out=earlier[:, :]).then_inc(earlier_rdy, 1)
                after(dve, earlier_rdy, k.n + 1)
                nc.vector.tensor_scalar(shift[:, :], earlier[:, :], 1.0, to_spare[:, bass.ds(k.n, 1)],
                                        ALU.min, ALU.mult).then_inc(shift_rdy, 1)
                after(dve, shift_rdy, k.n + 1)
                nc.vector.tensor_tensor(target[:, bass.ds(k.n, 1)], src_f[:, bass.ds(k.n, 1)], shift[:, :],
                                        ALU.add).then_inc(target_rdy, 1)

            def e_norm(k):
                p = k.place % 2
                after(dve, e_scale, k.n + 1)
                after(dve, edge_lo_rdy, k.n)
                nc.vector.tensor_scalar(edge_xn, edge_x[k.place], e_mv[p][:, 0:1], e_rv[p][:, :],
                                        ALU.subtract, ALU.mult).then_inc(edge_xn_rdy, 1)
                low_part(edge_lo[:, :], edge_xn, edge_hi[:, :], edge_hi_rdy, k.n + 1, edge_lo_rdy)

            def sumT_low(k):
                hi, lo = sumT[k.place % 2]
                low_part(lo[:, :, :], chunked(p_sumT[k.place % 2]), hi[:, :, :], sumT_hi, k.n + 1, sumT_lo)

            def edges(k):
                if k.plus(1).within(EDGE_TILES):
                    sumT_low(k.plus(1))
                if k.plus(2).within(EDGE_TILES):
                    same_target(k.plus(2))
                    e_norm(k.plus(2))
                if k.plus(3).within(EDGE_TILES):
                    e_moments_of(k.plus(3))

            e_moments_of(four(0))
            for k in range(-2, EDGE_SLOTS):
                edges(four(k))
            with dve.Fori(1, EDGE_TILES // EDGE_SLOTS - 1) as q:
                for place in range(EDGE_SLOTS):
                    edges(At(q, place, EDGE_SLOTS))
            for k in range(EDGE_TILES - EDGE_SLOTS, EDGE_TILES):
                edges(four(k))

            weight_lo(WW)
            weight_lo(WV)
            low_part(wgp[1][:, :, :], wg_raw[:, :, :], wgp[0][:, :, :], wg_hi, 1, wg_lo)
            weight_lo(WO)

            def mix(u):
                after(dve, agg_ld[u.place], 16 * (u.turn + 1))
                trans = t_ring[:, u.n % LEAD, :]
                nc.vector.scalar_tensor_tensor(diff, agg_in[u.place], 0.0, trans, ALU.max,
                                               ALU.subtract).then_inc(diff_rdy, 1)
                after(dve, gate_tanh, u.n + 1)
                after(dve, diff_rdy, u.n + 1)
                nc.vector.scalar_tensor_tensor(diff, g_ring[:, u.n % LEAD, :], 1.0, diff, ALU.add,
                                               ALU.mult).then_inc(gated_rdy, 1)
                after(dve, gated_rdy, u.n + 1)
                nc.vector.scalar_tensor_tensor(mixed, diff, 0.5, trans, ALU.mult,
                                               ALU.add).then_inc(mixed_rdy, 1)

            def b_moments_of(u):
                after(dve, x1_rdy, u.n + 1)
                nc.vector.bn_stats(b_st[:, :], x_ring[:, u.n % X_RING, :]).then_inc(b_stats, 1)
                after_apart(dve, (b_stats, u.n + 1))
                nc.vector.bn_aggr(b_mv[:, :], b_st[:, :]).then_inc(b_moments, 1)

            def b_norm(u):
                after(dve, x1nT_ps, u.n)
                after(dve, b_rstd, u.n + 1)
                nc.vector.tensor_scalar(x1n, x_ring[:, u.n % X_RING, :], b_mv[:, 0:1], b_rs[:, :],
                                        ALU.subtract, ALU.mult).then_inc(x1n_rdy, 1)

            def x1nT_low(u):
                low_part(x1nT[1], chunked(p_x1nT), x1nT[0], x1nT_hi, u.n + 1, x1nT_lo)

            def hT_low(v):
                low_part(hT[1], chunked(p_xnT_hT), hT[0], hT_hi, v.n + 1, hT_lo)

            def activate(u):
                after(dve, h_rdy, u.n)
                after(dve, z_tanh_rdy, u.n + 1)
                nc.vector.scalar_tensor_tensor(act, z_tanh, 1.0, p_zw[:, :], ALU.add,
                                               ALU.mult).then_inc(silu_rdy, 1)
                after(dve, zv_ps, u.n + 1)
                after(dve, silu_rdy, u.n + 1)
                nc.vector.tensor_tensor(act, act, p_zv[:, :], ALU.mult).then_inc(act_rdy, 1)

            def logits(u):
                nc.vector.tensor_copy(logit[:, :], p_logit[:, 0:NE]).then_inc(logit_rdy, 1)
                after_apart(dve, (logit_rdy, u.n + 1))
                nc.vector.max(best[:, :], logit[:, :]).then_inc(best_rdy, 1)
                after_apart(dve, (best_rdy, u.n + 1))
                nc.vector.max_index(best_i[:, :], best[:, :], logit[:, :]).then_inc(best_i_rdy, 1)
                nc.vector.tensor_tensor(gap[:, :], best[:, 1:2], best[:, 0:1], ALU.subtract).then_inc(gap_rdy, 1)
                after(dve, best_i_rdy, u.n + 1)
                nc.vector.tensor_copy(best_f[:, :], best_i[:, 0:2]).then_inc(best_f_rdy, 1)

            def shares(u):
                after(dve, e2_rdy, u.n + 1)
                nc.vector.tensor_scalar(total[:, :], e2[:, :], 1.0, 2.0, ALU.add, ALU.mult).then_inc(total_rdy, 1)
                after(dve, total_rdy, u.n + 1)
                nc.vector.reciprocal(share[:, 0:1], total[:, :]).then_inc(share1_rdy, 1)
                after(dve, share1_rdy, u.n + 1)
                nc.vector.tensor_tensor(share[:, 1:2], share[:, 0:1], e2[:, :], ALU.mult).then_inc(share2_rdy, 1)
                after(dve, best_f_rdy, u.n + 1)
                nc.vector.tensor_scalar(gw1[:, :], expert_f[:, :], best_f[:, 0:1], share[:, 0:1],
                                        ALU.is_equal, ALU.mult).then_inc(gw12_rdy, 1)
                after(dve, share2_rdy, u.n + 1)
                nc.vector.tensor_scalar(gw2[:, :], expert_f[:, :], best_f[:, 1:2], share[:, 1:2],
                                        ALU.is_equal, ALU.mult).then_inc(gw12_rdy, 1)
                after(dve, h_rdy, u.n)
                after(dve, gw12_rdy, 2 * u.n + 2)
                nc.vector.tensor_tensor(gw[:, :], gw1[:, :], gw2[:, :], ALU.add).then_inc(gw_rdy, 1)

            def residual(v):
                after(dve, out_st[v.place], 16 * v.turn)
                after(dve, y_ps, v.n + 1)
                nc.vector.tensor_tensor(out_sb[v.place], p_y[:, :], x_ring[:, v.n % X_RING, :],
                                        ALU.add).then_inc(out_rdy, 1)

            def rows(u):
                t = u.plus(LEAD)
                if u.plus(-1).within(TILES):
                    hT_low(u.plus(-1))
                if t.within(TILES):
                    xnT_low(t)
                activate(u)
                logits(u)
                if u.plus(1).within(TILES):
                    x1nT_low(u.plus(1))
                shares(u)
                if u.plus(-1).within(TILES):
                    residual(u.plus(-1))
                if u.plus(2).within(TILES):
                    mix(u.plus(2))
                if t.plus(1).within(TILES):
                    a_moments_of(t.plus(1))
                if t.within(TILES):
                    gate_bias(t)
                if t.plus(1).within(TILES):
                    a_norm(t.plus(1))
                if u.plus(2).within(TILES):
                    b_moments_of(u.plus(2))
                if t.within(TILES):
                    trans_bias(t)
                if u.plus(2).within(TILES):
                    b_norm(u.plus(2))

            for u in range(2):
                mix(pair(u))
                b_moments_of(pair(u))
                b_norm(pair(u))
                if u == 0:
                    x1nT_low(pair(0))
            for u in range(4):
                rows(pair(u))
            with dve.Fori(2, (TILES - LEAD) // 2 - 1) as i:
                rows(At(i, 0, 2))
                rows(At(i, 1, 2))
            for u in range(TILES - LEAD - 2, TILES):
                rows(pair(u))
            hT_low(pair(TILES - 1))
            residual(pair(TILES - 1))

        @block.tensor
        def _(pe):
            def product(ps, lhsT, rhs):
                terms = [(lhsT[a], rhs[b], c) for c in range(C) for a, b in ((0, 0), (0, 1), (1, 0))]
                for n, (a, b, c) in enumerate(terms):
                    last = nc.tensor.matmul(ps, a[:, c, :], b[:, c, :], start=n == 0, stop=n == len(terms) - 1)
                return last

            def transposed(ps, rows):
                for c in range(C):
                    last = nc.tensor.transpose(ps[:, c * P:(c + 1) * P], rows[:, c * P:(c + 1) * P], ident[:, :])
                return last

            def xn_transpose(t, v):
                if v is not None:
                    after(pe, hT_lo, v.n + 1)
                after(pe, xnT_lo, t.n)
                after(pe, xn_rdy, t.n + 1)
                transposed(p_xnT_hT, xn).then_inc(xnT_ps, 1)

            def gate_product(t):
                after(pe, gate_sb, t.n)
                after(pe, xnT_lo, t.n + 1)
                product(p_gate[:, :], xnT[t.place], w3p).then_inc(gate_ps, 1)

            def trans_product(t):
                after(pe, trans_sb, t.n)
                product(p_trans[:, :], xnT[t.place], w2p).then_inc(trans_ps, 1)

            pe.wait_ge(ident_rdy, 1)
            xn_transpose(pair(0), None)
            pe.wait_ge(w_lo, W3 + 1)

            def ahead(t):
                gate_product(t)
                if not (isinstance(t.n, int) and t.n == LEAD - 1):
                    xn_transpose(t.plus(1), None)
                trans_product(t)

            gate_product(pair(0))
            xn_transpose(pair(1), None)
            pe.wait_ge(w_lo, W2 + 1)
            trans_product(pair(0))
            ahead(pair(1))
            with pe.Fori(1, LEAD // 2) as i:
                ahead(At(i, 0, 2))
                ahead(At(i, 1, 2))
            ahead(pair(LEAD - 1))

            def sums(k):
                p = k.place % 2
                after(pe, sumT_lo, k.n - 1)
                after(pe, same_rdy, k.n + 1)
                after(pe, edge_lo_rdy, k.n + 1)
                for c in range(C):
                    cols = slice(c * P, (c + 1) * P)
                    nc.tensor.matmul(p_sumT[p][:, cols], edge_hi[:, cols], same[:, :], start=True, stop=False)
                    last = nc.tensor.matmul(p_sumT[p][:, cols], edge_lo[:, cols], same[:, :],
                                            start=False, stop=True)
                last.then_inc(sumT_ps, 1)

            def messages(k):
                p = k.place % 2
                after(pe, msg_sb, k.n - 1)
                after(pe, sumT_lo, k.n + 1)
                product(p_msg[p][:, :], sumT[p], w1O).then_inc(msg_ps, 1)

            def edges(k):
                if k.plus(1).within(EDGE_TILES):
                    sums(k.plus(1))
                if k.within(EDGE_TILES):
                    messages(k)

            edges(four(-1))
            pe.wait_ge(w_lo, W1 + 1)
            for k in range(EDGE_SLOTS):
                edges(four(k))
            with pe.Fori(1, EDGE_TILES // EDGE_SLOTS - 1) as q:
                for place in range(EDGE_SLOTS):
                    edges(At(q, place, EDGE_SLOTS))
            for k in range(EDGE_TILES - EDGE_SLOTS, EDGE_TILES):
                edges(four(k))

            def x1n_transpose(u):
                after(pe, x1nT_lo, u.n)
                after(pe, x1n_rdy, u.n + 1)
                transposed(p_x1nT, x1n).then_inc(x1nT_ps, 1)

            def experts_in(u):
                after(pe, x1nT_lo, u.n + 1)
                after(pe, logit_rdy, u.n)
                product(p_logit[:, 0:NE], x1nT, wgp)
                after(pe, silu_rdy, u.n)
                product(p_zw[:, :], x1nT, wWp).then_inc(zw_ps, 1)
                after(pe, act_rdy, u.n)
                product(p_zv[:, :], x1nT, wVp).then_inc(zv_ps, 1)

            def h_transpose(u):
                t = u.plus(LEAD)
                if t.within(TILES):
                    after(pe, xnT_lo, t.n + 1)
                after(pe, hT_lo, u.n)
                after(pe, h_rdy, u.n + 1)
                transposed(p_xnT_hT, h).then_inc(hT_ps, 1)

            def experts_out(v):
                after(pe, out_rdy, v.n)
                after(pe, hT_lo, v.n + 1)
                product(p_y[:, :], hT, w1O).then_inc(y_ps, 1)

            def rows(u):
                t = u.plus(LEAD)
                experts_in(u)
                if t.within(TILES):
                    xn_transpose(t, u.plus(-1))
                if u.plus(1).within(TILES):
                    x1n_transpose(u.plus(1))
                if u.plus(-1).within(TILES):
                    experts_out(u.plus(-1))
                if t.within(TILES):
                    gate_product(t)
                    trans_product(t)
                h_transpose(u)

            x1n_transpose(pair(0))
            pe.wait_ge(wg_lo, 1)
            pe.wait_ge(w_lo, len(weights))
            rows(pair(0))
            rows(pair(1))
            with pe.Fori(1, (TILES - LEAD) // 2 - 1) as i:
                rows(At(i, 0, 2))
                rows(At(i, 1, 2))
            for u in range(TILES - LEAD - 2, TILES):
                rows(pair(u))
            experts_out(pair(TILES - 1))


def kernel(x, src, dst, edge_weight, L0_gnn_w1, L0_gnn_w2, L0_gnn_w3, L0_gnn_b1, L0_gnn_b2, L0_gnn_b3,
           L0_ffn_Wg, L0_ffn_W, L0_ffn_V, L0_ffn_W2):
    import numpy as np
    import concourse.bacc as bacc
    from concourse.bass_utils import run_bass_kernel_spmd

    rows, d = x.shape
    padded = -(-rows // P) * P
    edge_rows = EDGE_SLOTS * P
    edges = -(-len(src) // edge_rows) * edge_rows
    if padded == rows:
        padded += P

    xp = np.zeros((padded, d), x.dtype)
    xp[:rows] = x
    srcp = np.full(edges, padded - 1, src.dtype)
    srcp[:len(src)] = src
    dstp = np.zeros(edges, dst.dtype)
    dstp[:len(dst)] = dst
    valp = np.zeros(edges, edge_weight.dtype)
    valp[:len(edge_weight)] = edge_weight

    def columns(a):
        return np.ascontiguousarray(np.asarray(a).reshape(-1, P).T)

    def experts_side_by_side(w):
        return np.ascontiguousarray(np.transpose(np.asarray(w), (1, 0, 2)).reshape(d, -1))

    arrays = {
        "x": xp, "src_rows": srcp, "src_cols": columns(srcp), "dst_cols": columns(dstp),
        "val_cols": columns(valp), "w1": L0_gnn_w1, "w2": L0_gnn_w2, "w3": L0_gnn_w3,
        "b1": L0_gnn_b1, "b2": L0_gnn_b2, "b3": L0_gnn_b3, "wg": L0_ffn_Wg,
        "wW": experts_side_by_side(L0_ffn_W), "wV": experts_side_by_side(L0_ffn_V),
        "wO": np.asarray(L0_ffn_W2).reshape(-1, d),
    }
    arrays = {k: np.ascontiguousarray(v) for k, v in arrays.items()}
    nc = bacc.Bacc("TRN2", target_bir_lowering=False, num_devices=1)
    ins = {k: nc.dram_tensor("in_" + k, v.shape, mybir.dt.from_np(v.dtype), kind="ExternalInput").ap()
           for k, v in arrays.items()}
    out = nc.dram_tensor("out_rows", (padded, d), F32, kind="ExternalOutput").ap()
    gnn_experts_kernel(nc, **ins, out=out)
    r = run_bass_kernel_spmd(nc, [{"in_" + k: v for k, v in arrays.items()}], core_ids=[0])
    return r.results[0]["out_rows"][:rows]
```

```python
from contextlib import ExitStack

import concourse.bass as bass
from concourse import mybir

F32 = mybir.dt.float32
F32R = mybir.dt.float32r
I32 = mybir.dt.int32
U32 = mybir.dt.uint32
ALU = mybir.AluOpType
ACT = mybir.ActivationFunctionType

P = 128
LEAD = 9
EPS = 1e-5
EDGE_SLOTS = 4


class At:

    def __init__(self, turn, place, unroll):
        self.turn, self.place, self.unroll = turn, place, unroll
        self.n = turn * unroll + place

    def plus(self, k):
        turns, place = divmod(self.place + k, self.unroll)
        return At(self.turn + turns, place, self.unroll)

    def within(self, count):
        return not isinstance(self.n, int) or 0 <= self.n < count

    def beyond(self, count):
        return isinstance(self.n, int) and self.n >= count

    def is_first(self):
        return isinstance(self.n, int) and self.n == 0


def pair(n):
    return At(n // 2, n % 2, 2)


def four(n):
    return At(n // EDGE_SLOTS, n % EDGE_SLOTS, EDGE_SLOTS)


def after(eng, sem, count):
    if not isinstance(count, int) or count > 0:
        eng.wait_ge(sem, count)


def after_apart(eng, *waits):
    if isinstance(waits[0][1], int):
        for sem, count in waits:
            after(eng, sem, count)
        return
    counts = [eng.snap(count) for _, count in waits]
    for count in counts:
        eng.compute_val(count)
    eng.wait_ge(waits[0][0], 1)
    for (sem, _), count in zip(waits, counts):
        eng.wait_ge(sem, count)


def gnn_experts_kernel(nc, x, src_rows, src_cols, dst_cols, val_cols, w1, w2, w3, b1, b2, b3,
                       wg, wW, wV, wO, out):
    ROWS, D = x.shape
    TILES = ROWS // P
    C = D // P
    EDGE_TILES = src_cols.shape[1]
    NE = wg.shape[1]
    FE = D // NE
    SPARE = ROWS
    X_RING = LEAD + 4
    FILL_ROWS = 512
    FILLS = (ROWS + P) // FILL_ROWS
    assert D == 512 and ROWS % P == 0 and (TILES - LEAD) % 2 == 0 and LEAD % 2 == 1
    assert EDGE_TILES % EDGE_SLOTS == 0 and (ROWS + P) % FILL_ROWS == 0 and FILLS >= 2 * LEAD + 2

    agg = nc.dram_tensor("agg", (ROWS + P, D), F32, kind="Internal").ap()

    with ExitStack() as ctx:
        def sb(name, shape, dt=F32):
            return ctx.enter_context(nc.sbuf_tensor(name, shape, dt))

        def sem(name):
            return ctx.enter_context(nc.semaphore(name))

        ident = sb("ident", [P, P])
        before = sb("before", [P, P])
        minus_half = sb("minus_half", [P, 1])
        expert_i = sb("expert_i", [P, NE], I32)
        expert_f = sb("expert_f", [P, NE])
        spare_i = sb("spare_i", [P, 1], I32)
        spare_f = sb("spare_f", [P, 1])
        b2_all = sb("b2_all", [P, D])
        b3_all = sb("b3_all", [P, D])

        stage = [sb(f"stage{i}", [P, C, D]) for i in range(2)]
        def parts(name, n=D):
            return sb(name + "_hi", [P, C, n], F32R), sb(name + "_lo", [P, C, n], F32R)
        w1O = parts("w1_then_wO")
        w2p, w3p, wWp, wVp = parts("w2"), parts("w3"), parts("wW"), parts("wV")
        wg_parts = sb("wg_parts", [P, C, 2 * NE], F32R)
        wg_raw = sb("wg_raw", [P, C, NE])
        weights = [(w3, w3p), (w2, w2p), (w1, w1O), (wW, wWp), (wV, wVp), (wO, w1O)]
        W3, W2, W1, WW, WV, WO = range(len(weights))

        x_ring = sb("x_ring", [P, X_RING, D])
        t_ring = sb("t_ring", [P, LEAD, D])
        g_ring = sb("g_ring", [P, LEAD, D])
        xn = sb("xn", [P, D])
        xnT = [(sb(f"xnT_hi{i}", [P, C, P], F32R), sb(f"xnT_lo{i}", [P, C, P], F32R)) for i in range(2)]
        a_st = sb("a_st", [P, 6])
        a_mv = sb("a_mv", [P, 2])
        a_rs = sb("a_rs", [P, 1])

        work = sb("work", [P, 10, D])
        edge_x = [work[:, i, :] for i in range(4)]
        edge_xn = work[:, 4, :]
        edge_msg = [work[:, 5 + i, :] for i in range(4)]
        b1_all = work[:, 9, :]
        agg_in = [work[:, i, :] for i in range(2)]
        diff, mixed, x1n, z_tanh, act, h = (work[:, 2 + i, :] for i in range(6))
        out_sb = [work[:, 8 + i, :] for i in range(2)]

        workr = [sb(f"workr{i}", [P, D], F32R) for i in range(4)]
        edge_hi, edge_lo = workr[0], workr[1]
        def chunked(a):
            return a[:, :].rearrange("p (c m) -> p c m", c=C)
        x1nT = (chunked(workr[0]), chunked(workr[1]))
        hT = (chunked(workr[2]), chunked(workr[3]))
        sumT = xnT

        same = [sb(f"same{i}", [P, P], F32R) for i in range(2)]
        same_before = sb("same_before", [P, P])
        src_row = [sb(f"src_row{i}", [P, P], I32) for i in range(4)]
        src_i = sb("src_i", [P, EDGE_TILES], I32)
        dst_i = sb("dst_i", [P, EDGE_TILES], I32)
        val = sb("val", [P, EDGE_TILES])
        src_f = sb("src_f", [P, EDGE_TILES])
        to_spare = sb("to_spare", [P, EDGE_TILES])
        target = sb("target", [P, EDGE_TILES], I32)
        dst_idx = [sb(f"dst_idx{i}", [P, 1], I32) for i in range(4)]
        src_idx = [sb(f"src_idx{i}", [P, 1], I32) for i in range(4)]
        earlier = sb("earlier", [P, 1])
        shift = sb("shift", [P, 1])
        e_st = sb("e_st", [P, 6])
        e_mv = [sb(f"e_mv{i}", [P, 2]) for i in range(2)]
        e_rs = [sb(f"e_rs{i}", [P, 1]) for i in range(2)]
        e_rv = [sb(f"e_rv{i}", [P, 1]) for i in range(2)]

        b_st = sb("b_st", [P, 6])
        b_mv = sb("b_mv", [P, 2])
        b_rs = sb("b_rs", [P, 1])
        logit_parts_T = sb("logit_parts_T", [2 * NE, P])
        logit_parts = sb("logit_parts", [P, 2 * NE])
        logit = sb("logit", [P, NE])
        best = sb("best", [P, 8])
        best_i = sb("best_i", [P, 8], U32)
        best_f = sb("best_f", [P, 2])
        gap = sb("gap", [P, 1])
        e2 = sb("e2", [P, 1])
        total = sb("total", [P, 1])
        share = sb("share", [P, 2])
        gw1 = sb("gw1", [P, NE])
        gw2 = sb("gw2", [P, NE])
        gw = sb("gw", [P, NE])

        bank = [ctx.enter_context(nc.psum_tensor(f"bank{i}", [P, D], F32)) for i in range(8)]
        p_xnT_hT, p_x1nT, p_gate, p_trans, p_zw, p_zv, p_y, p_logit = bank
        p_sumT = [p_zw, p_zv]
        p_msg = [p_y, p_logit]
        p_logit_T = p_logit[0:2 * NE, 0:P]
        p_logit_rows = p_logit[:, P:P + 2 * NE]

        consts_ld = sem("consts_ld")
        edges_ld = sem("edges_ld")
        b1_ld = sem("b1_ld")
        filled = sem("filled")
        stage_ld = [sem(f"stage_ld{i}") for i in range(2)]
        wg_ld = sem("wg_ld")
        w_hi = sem("w_hi")
        w_lo = sem("w_lo")
        wg_hi = sem("wg_hi")
        wg_lo = sem("wg_lo")
        memset_done = sem("memset_done")
        ident_rdy = sem("ident_rdy")
        before_rdy = sem("before_rdy")
        iota_rdy = sem("iota_rdy")
        spare_rdy = sem("spare_rdy")
        expert_rdy = sem("expert_rdy")
        src_f_rdy = sem("src_f_rdy")
        to_spare_rdy = sem("to_spare_rdy")

        x_ld = [sem(f"x_ld{i}") for i in range(2)]
        a_stats = sem("a_stats")
        a_moments = sem("a_moments")
        a_var = sem("a_var")
        a_rstd = sem("a_rstd")
        xn_rdy = sem("xn_rdy")
        xnT_ps = sem("xnT_ps")
        xnT_hi = sem("xnT_hi")
        xnT_lo = sem("xnT_lo")
        gate_ps = sem("gate_ps")
        trans_ps = sem("trans_ps")
        gate_sb = sem("gate_sb")
        gate_tanh = sem("gate_tanh")
        trans_sb = sem("trans_sb")

        src_row_ld = [sem(f"src_row_ld{i}") for i in range(4)]
        dst_idx_rdy = sem("dst_idx_rdy")
        gathered = [sem(f"gathered{i}") for i in range(4)]
        same_rdy = sem("same_rdy")
        earlier_rdy = sem("earlier_rdy")
        shift_rdy = sem("shift_rdy")
        target_rdy = sem("target_rdy")
        e_stats = sem("e_stats")
        e_moments = sem("e_moments")
        e_var = sem("e_var")
        e_rstd = sem("e_rstd")
        e_scale = sem("e_scale")
        edge_xn_rdy = sem("edge_xn_rdy")
        edge_hi_rdy = sem("edge_hi_rdy")
        edge_lo_rdy = sem("edge_lo_rdy")
        sumT_ps = sem("sumT_ps")
        sumT_hi = sem("sumT_hi")
        sumT_lo = sem("sumT_lo")
        msg_ps = sem("msg_ps")
        msg_sb = sem("msg_sb")
        src_idx_rdy = sem("src_idx_rdy")
        added = sem("added")

        agg_ld = [sem(f"agg_ld{i}") for i in range(2)]
        diff_rdy = sem("diff_rdy")
        gated_rdy = sem("gated_rdy")
        mixed_rdy = sem("mixed_rdy")
        x1_rdy = sem("x1_rdy")
        b_stats = sem("b_stats")
        b_moments = sem("b_moments")
        b_var = sem("b_var")
        b_rstd = sem("b_rstd")
        x1n_rdy = sem("x1n_rdy")
        x1nT_ps = sem("x1nT_ps")
        x1nT_hi = sem("x1nT_hi")
        x1nT_lo = sem("x1nT_lo")
        zw_ps = sem("zw_ps")
        zv_ps = sem("zv_ps")
        z_tanh_rdy = sem("z_tanh_rdy")
        silu_rdy = sem("silu_rdy")
        act_rdy = sem("act_rdy")
        logit_T_ps = sem("logit_T_ps")
        logit_T_sb = sem("logit_T_sb")
        logit_ps = sem("logit_ps")
        logit_parts_rdy = sem("logit_parts_rdy")
        logit_rdy = sem("logit_rdy")
        best_rdy = sem("best_rdy")
        best_i_rdy = sem("best_i_rdy")
        gap_rdy = sem("gap_rdy")
        best_f_rdy = sem("best_f_rdy")
        e2_rdy = sem("e2_rdy")
        total_rdy = sem("total_rdy")
        share1_rdy = sem("share1_rdy")
        share2_rdy = sem("share2_rdy")
        gw12_rdy = sem("gw12_rdy")
        gw_rdy = sem("gw_rdy")
        h_rdy = sem("h_rdy")
        hT_ps = sem("hT_ps")
        hT_hi = sem("hT_hi")
        hT_lo = sem("hT_lo")
        y_ps = sem("y_ps")
        out_rdy = sem("out_rdy")
        out_st = [sem(f"out_st{i}") for i in range(2)]

        block = ctx.enter_context(nc.Block())

        @block.sync
        def _(sp):
            def load_weight(i):
                after(sp, w_lo, i - 1)
                sp.dma_start(stage[i % 2][:, :, :],
                             weights[i][0].rearrange("(c p) n -> p c n", p=P)).then_inc(stage_ld[i % 2], 16)

            def load_x(t):
                sp.dma_start(x_ring[:, t.n % X_RING, :], x[bass.ds(t.n * P, P), :]).then_inc(x_ld[t.place], 16)

            def fill(i):
                sp.dma_start(agg[i * FILL_ROWS:(i + 1) * FILL_ROWS, :].rearrange("(a p) d -> p a d", p=P),
                             b1_all.unsqueeze(1).to_broadcast([P, FILL_ROWS // P, D])).then_inc(filled, 16)

            def load_src_row(k):
                after(sp, same_rdy, k.n - EDGE_SLOTS + 1)
                sp.dma_start(src_row[k.place][:, :],
                             src_rows[bass.ds(k.n * P, P)].partition_broadcast(P)).then_inc(src_row_ld[k.place], 16)

            def load_agg(u):
                sp.dma_start(agg_in[u.place], agg[bass.ds(u.n * P, P), :]).then_inc(agg_ld[u.place], 16)

            load_x(pair(0))
            load_weight(W3)
            sp.dma_start(b1_all, b1.partition_broadcast(P)).then_inc(b1_ld, 16)
            load_weight(W2)
            load_x(pair(1))
            sp.dma_start(b3_all[:, :], b3.partition_broadcast(P)).then_inc(consts_ld, 16)
            sp.dma_start(b2_all[:, :], b2.partition_broadcast(P)).then_inc(consts_ld, 16)
            for edge_in, at in ((src_i, src_cols), (dst_i, dst_cols), (val, val_cols)):
                sp.dma_start(edge_in[:, :], at).then_inc(edges_ld, 16)
            sp.wait_ge(b1_ld, 16)
            fill(0)
            fill(1)
            for t in range(LEAD):
                after(sp, a_stats, t + 1)
                load_x(pair(t + 2))
                if t == 2:
                    load_weight(W1)
                if t == 3:
                    for k in range(EDGE_SLOTS):
                        load_src_row(four(k))
                for i in range(2 * t + 2, min(2 * t + 4, FILLS)):
                    fill(i)
            for i in range(2 * LEAD + 2, FILLS):
                fill(i)

            for k in range(EDGE_SLOTS, 2 * EDGE_SLOTS):
                load_src_row(four(k))
            load_weight(WW)
            sp.dma_start(wg_raw[:, :, :], wg.rearrange("(c p) n -> p c n", p=P)).then_inc(wg_ld, 16)
            load_weight(WV)
            with sp.Fori(2, EDGE_TILES // EDGE_SLOTS) as q:
                for place in range(EDGE_SLOTS):
                    load_src_row(At(q, place, EDGE_SLOTS))

            sp.wait_ge(added, 16 * EDGE_TILES)
            load_agg(pair(0))
            load_agg(pair(1))
            load_weight(WO)
            sp.wait_ge(mixed_rdy, 1)
            load_agg(pair(2))

            def rows(u):
                t = u.plus(LEAD)
                if u.plus(3).within(TILES):
                    after(sp, mixed_rdy, u.n + 2)
                    load_agg(u.plus(3))
                if t.plus(2).within(TILES):
                    after_apart(sp, (a_stats, t.n + 1), (out_rdy, u.n - 1))
                    load_x(t.plus(2))
                if u.plus(-1).within(TILES):
                    store_out(u.plus(-1))

            def store_out(v):
                after(sp, out_rdy, v.n + 1)
                sp.dma_start(out[bass.ds(v.n * P, P), :], out_sb[v.place]).then_inc(out_st[v.place], 16)

            rows(pair(0))
            rows(pair(1))
            with sp.Fori(1, (TILES - LEAD) // 2 - 1) as i:
                rows(At(i, 0, 2))
                rows(At(i, 1, 2))
            for u in range(TILES - LEAD - 2, TILES):
                rows(pair(u))
            store_out(pair(TILES - 1))
            for place in range(2):
                sp.wait_ge(out_st[place], 16 * ((TILES + 1 - place) // 2))

        @block.gpsimd
        def _(pool):
            nc.gpsimd.memset(ident[:, :], 0.0).then_inc(memset_done, 1)
            nc.gpsimd.memset(before[:, :], 1.0).then_inc(memset_done, 1)
            nc.gpsimd.iota(expert_i[:, :], pattern=[[1, NE]], base=0, channel_multiplier=0).then_inc(iota_rdy, 1)
            nc.gpsimd.iota(spare_i[:, :], pattern=[[1, 1]], base=SPARE, channel_multiplier=1).then_inc(iota_rdy, 1)
            nc.gpsimd.memset(minus_half[:, :], -0.5).then_inc(memset_done, 1)
            pool.wait_ge(memset_done, 3)
            nc.gpsimd.affine_select(out=ident[:, :], in_=ident[:, :], compare_op=ALU.not_equal, fill=1.0,
                                    base=0, pattern=[[-1, P]], channel_multiplier=1).then_inc(ident_rdy, 1)
            nc.gpsimd.affine_select(out=before[:, :], in_=before[:, :], compare_op=ALU.is_gt, fill=0.0,
                                    base=0, pattern=[[-1, P]], channel_multiplier=1).then_inc(before_rdy, 1)

            def rstd(mv, rs, moments, n, var_rdy, done):
                after_apart(pool, (moments, n + 1))
                nc.gpsimd.tensor_scalar(rs[:, :], mv[:, 1:2], EPS, None, ALU.add).then_inc(var_rdy, 1)
                after(pool, var_rdy, n + 1)
                nc.gpsimd.tensor_tensor(rs[:, :], rs[:, :], minus_half[:, :], ALU.pow).then_inc(done, 1)

            def gather(k):
                after_apart(pool, (dst_idx_rdy, k.n + 1), (edge_xn_rdy, k.n - EDGE_SLOTS + 1))
                pool.indirect_dma_start(
                    out=edge_x[k.place], out_offset=None, in_=x,
                    in_offset=bass.IndirectOffsetOnAxis(ap=dst_idx[k.place][:, 0:1], axis=0),
                ).then_inc(gathered[k.place], 16)

            rstd(a_mv, a_rs, a_moments, 0, a_var, a_rstd)
            with pool.Fori(0, LEAD - EDGE_SLOTS) as t:
                rstd(a_mv, a_rs, a_moments, t + 1, a_var, a_rstd)
            for k in range(EDGE_SLOTS):
                gather(four(k))
                rstd(a_mv, a_rs, a_moments, LEAD - EDGE_SLOTS + k + 1, a_var, a_rstd)


            def edge_rstd(k):
                p = k.place % 2
                after(pool, e_var, k.n + 1)
                nc.gpsimd.tensor_tensor(e_rs[p][:, :], e_mv[p][:, 1:2], minus_half[:, :],
                                        ALU.pow).then_inc(e_rstd, 1)

            def edges(k):
                if k.plus(6).within(EDGE_TILES):
                    gather(k.plus(6))
                if k.plus(4).within(EDGE_TILES):
                    edge_rstd(k.plus(4))
                after_apart(pool, (src_idx_rdy, k.n + 1), (msg_sb, k.n + 1), (added, k.n * 16))
                pool.indirect_dma_start(
                    out=agg, out_offset=bass.IndirectOffsetOnAxis(ap=src_idx[k.place][:, 0:1], axis=0),
                    in_=edge_msg[k.place], in_offset=None, bounds_check=ROWS + P - 1, compute_op=ALU.add,
                ).then_inc(added, 16)

            for k in range(4):
                edge_rstd(four(k))
            for k in (4, 5):
                gather(four(k))
            pool.wait_ge(filled, 16 * FILLS)
            for k in range(EDGE_SLOTS):
                edges(four(k))
            with pool.Fori(1, EDGE_TILES // EDGE_SLOTS - 2) as q:
                for place in range(EDGE_SLOTS):
                    edges(At(q, place, EDGE_SLOTS))
            for k in range(EDGE_TILES - 2 * EDGE_SLOTS, EDGE_TILES):
                edges(four(k))

            def x1(u):
                after(pool, mixed_rdy, u.n + 1)
                ring = x_ring[:, u.n % X_RING, :]
                nc.gpsimd.tensor_tensor(ring, mixed, ring, ALU.add).then_inc(x1_rdy, 1)

            def rows(u):
                t = u.plus(LEAD)
                if t.beyond(TILES) and u.plus(2).within(TILES):
                    x1(u.plus(2))
                after(pool, hT_ps, u.n)
                after(pool, act_rdy, u.n + 1)
                after(pool, gw_rdy, u.n + 1)
                nc.gpsimd.tensor_tensor(
                    h.rearrange("p (e f) -> p e f", e=NE), act.rearrange("p (e f) -> p e f", e=NE),
                    gw[:, :].unsqueeze(2).to_broadcast([P, NE, FE]), ALU.mult).then_inc(h_rdy, 1)
                if t.within(TILES):
                    x1(u.plus(2))
                if t.plus(1).within(TILES):
                    rstd(a_mv, a_rs, a_moments, t.n + 1, a_var, a_rstd)
                if u.plus(2).within(TILES):
                    rstd(b_mv, b_rs, b_moments, u.n + 2, b_var, b_rstd)

            for u in range(2):
                x1(pair(u))
                rstd(b_mv, b_rs, b_moments, u, b_var, b_rstd)
            rows(pair(0))
            rows(pair(1))
            with pool.Fori(1, (TILES - LEAD) // 2 - 1) as i:
                rows(At(i, 0, 2))
                rows(At(i, 1, 2))
            for u in range(TILES - LEAD - 2, TILES):
                rows(pair(u))

        @block.scalar
        def _(act_e):
            def weight_hi(i):
                act_e.wait_ge(stage_ld[i % 2], 16 * (i // 2 + 1))
                nc.scalar.activation(weights[i][1][0][:, :, :], stage[i % 2][:, :, :], ACT.Copy).then_inc(w_hi, 1)

            def xnT_high(t):
                after(act_e, trans_ps, t.n - 1)
                after(act_e, xnT_ps, t.n + 1)
                nc.scalar.activation(xnT[t.place][0][:, :, :], chunked(p_xnT_hT), ACT.Copy).then_inc(xnT_hi, 1)

            def gate_act(t):
                after(act_e, gate_sb, t.n + 1)
                ring = g_ring[:, t.n % LEAD, :]
                nc.scalar.activation(ring, ring, ACT.Tanh, scale=0.5).then_inc(gate_tanh, 1)

            def gather_index(k):
                after(act_e, gathered[k.place], 16 * k.turn)
                nc.scalar.activation(dst_idx[k.place][:, :], dst_i[:, bass.ds(k.n, 1)],
                                     ACT.Copy).then_inc(dst_idx_rdy, 1)

            weight_hi(W3)
            xnT_high(pair(0))
            weight_hi(W2)

            def ahead(t):
                xnT_high(t.plus(1))
                gate_act(t)

            ahead(pair(0))
            ahead(pair(1))
            act_e.wait_ge(edges_ld, 48)
            for k in range(EDGE_SLOTS):
                gather_index(four(k))
            with act_e.Fori(1, LEAD // 2) as i:
                ahead(At(i, 0, 2))
                ahead(At(i, 1, 2))
            weight_hi(W1)
            gate_act(pair(LEAD - 1))

            def edge_high(k):
                after(act_e, edge_xn_rdy, k.n + 1)
                after(act_e, sumT_ps, k.n)
                nc.scalar.activation(edge_hi[:, :], edge_xn, ACT.Copy).then_inc(edge_hi_rdy, 1)

            def sumT_high(k):
                after(act_e, sumT_ps, k.n + 1)
                after(act_e, msg_ps, k.n - 1)
                nc.scalar.activation(sumT[k.place % 2][0][:, :, :], chunked(p_sumT[k.place % 2]),
                                     ACT.Copy).then_inc(sumT_hi, 1)

            def message(k):
                after(act_e, added, (k.n - EDGE_SLOTS + 1) * 16)
                after(act_e, target_rdy, k.n + 1)
                nc.scalar.activation(src_idx[k.place][:, :], target[:, bass.ds(k.n, 1)],
                                     ACT.Copy).then_inc(src_idx_rdy, 1)
                after(act_e, msg_ps, k.n + 1)
                nc.scalar.activation(edge_msg[k.place], p_msg[k.place % 2][:, :], ACT.Copy).then_inc(msg_sb, 1)

            def edges(k):
                if k.plus(1).within(EDGE_TILES):
                    sumT_high(k.plus(1))
                if k.plus(2).within(EDGE_TILES):
                    edge_high(k.plus(2))
                if k.plus(6).within(EDGE_TILES):
                    gather_index(k.plus(6))
                if k.within(EDGE_TILES):
                    message(k)

            for k in range(-2, EDGE_SLOTS):
                edges(four(k))
            with act_e.Fori(1, EDGE_TILES // EDGE_SLOTS - 2) as q:
                for place in range(EDGE_SLOTS):
                    edges(At(q, place, EDGE_SLOTS))
            for k in range(EDGE_TILES - 2 * EDGE_SLOTS, EDGE_TILES):
                edges(four(k))

            xnT_high(pair(LEAD))
            weight_hi(WW)
            weight_hi(WV)
            act_e.wait_ge(wg_ld, 16)
            nc.scalar.activation(wg_parts[:, :, 0:NE], wg_raw[:, :, :], ACT.Copy).then_inc(wg_hi, 1)
            def x1nT_high(u):
                after(act_e, x1nT_ps, u.n + 1)
                nc.scalar.activation(x1nT[0], chunked(p_x1nT), ACT.Copy).then_inc(x1nT_hi, 1)

            def second_share(u):
                after(act_e, gap_rdy, u.n + 1)
                nc.scalar.activation(e2[:, :], gap[:, :], ACT.Exp).then_inc(e2_rdy, 1)

            def hT_high(v):
                after(act_e, hT_ps, v.n + 1)
                nc.scalar.activation(hT[0], chunked(p_xnT_hT), ACT.Copy).then_inc(hT_hi, 1)

            def rows(u):
                t = u.plus(LEAD)
                if u.plus(-1).within(TILES):
                    hT_high(u.plus(-1))
                after(act_e, logit_T_ps, u.n + 1)
                nc.scalar.activation(logit_parts_T[:, :], p_logit_T, ACT.Copy).then_inc(logit_T_sb, 1)
                after(act_e, silu_rdy, u.n)
                after(act_e, zw_ps, u.n + 1)
                nc.scalar.activation(z_tanh, p_zw[:, :], ACT.Tanh, scale=0.5).then_inc(z_tanh_rdy, 1)
                if t.beyond(TILES):
                    second_share(u)
                if t.within(TILES) and not u.is_first():
                    xnT_high(t)
                if u.plus(1).within(TILES):
                    x1nT_high(u.plus(1))
                if t.within(TILES):
                    second_share(u)
                if t.within(TILES):
                    gate_act(t)

            x1nT_high(pair(0))
            weight_hi(WO)
            rows(pair(0))
            rows(pair(1))
            with act_e.Fori(1, (TILES - LEAD) // 2 - 1) as i:
                rows(At(i, 0, 2))
                rows(At(i, 1, 2))
            for u in range(TILES - LEAD - 2, TILES):
                rows(pair(u))
            hT_high(pair(TILES - 1))

        @block.vector
        def _(dve):
            def f32(a):
                return a.bitcast(F32)

            def low_part(out, whole, high, have_high, count, done):
                after(dve, have_high, count)
                nc.vector.tensor_tensor(out, whole, f32(high), ALU.subtract).then_inc(done, 1)

            def weight_lo(i):
                hi, lo = weights[i][1]
                low_part(lo[:, :, :], stage[i % 2][:, :, :], hi[:, :, :], w_hi, i + 1, w_lo)

            def a_moments_of(t):
                after(dve, x_ld[t.place], 16 * (t.turn + 1))
                nc.vector.bn_stats(a_st[:, :], x_ring[:, t.n % X_RING, :]).then_inc(a_stats, 1)
                after_apart(dve, (a_stats, t.n + 1))
                nc.vector.bn_aggr(a_mv[:, :], a_st[:, :]).then_inc(a_moments, 1)

            def a_norm(t):
                after(dve, a_rstd, t.n + 1)
                nc.vector.tensor_scalar(xn[:, :], x_ring[:, t.n % X_RING, :], a_mv[:, 0:1], a_rs[:, :],
                                        ALU.subtract, ALU.mult).then_inc(xn_rdy, 1)

            def xnT_low(t):
                hi, lo = xnT[t.place]
                low_part(lo[:, :, :], chunked(p_xnT_hT), hi[:, :, :], xnT_hi, t.n + 1, xnT_lo)

            def gate_bias(t):
                after(dve, gate_ps, t.n + 1)
                nc.vector.tensor_tensor(g_ring[:, t.n % LEAD, :], p_gate[:, :], b3_all[:, :],
                                        ALU.add).then_inc(gate_sb, 1)

            def trans_bias(t):
                after(dve, trans_ps, t.n + 1)
                nc.vector.tensor_tensor(t_ring[:, t.n % LEAD, :], p_trans[:, :], b2_all[:, :],
                                        ALU.add).then_inc(trans_sb, 1)

            a_moments_of(pair(0))
            a_norm(pair(0))
            weight_lo(W3)
            xnT_low(pair(0))
            weight_lo(W2)
            dve.wait_ge(consts_ld, 32)

            def ahead(t):
                a_moments_of(t.plus(1))
                a_norm(t.plus(1))
                gate_bias(t)
                if not (isinstance(t.n, int) and t.n == LEAD - 1):
                    xnT_low(t.plus(1))
                trans_bias(t)

            with dve.Fori(0, LEAD // 2) as i:
                ahead(At(i, 0, 2))
                ahead(At(i, 1, 2))

            dve.wait_ge(iota_rdy, 2)
            nc.vector.tensor_copy(spare_f[:, :], spare_i[:, :]).then_inc(spare_rdy, 1)
            nc.vector.tensor_copy(expert_f[:, :], expert_i[:, :]).then_inc(expert_rdy, 1)
            dve.wait_ge(edges_ld, 48)
            nc.vector.tensor_copy(src_f[:, :], src_i[:, :]).then_inc(src_f_rdy, 1)
            dve.wait_ge(spare_rdy, 1)
            dve.wait_ge(src_f_rdy, 1)
            nc.vector.tensor_scalar(to_spare[:, :], src_f[:, :], -1.0, spare_f[:, :],
                                    ALU.mult, ALU.add).then_inc(to_spare_rdy, 1)
            dve.wait_ge(to_spare_rdy, 1)
            dve.wait_ge(before_rdy, 1)
            weight_lo(W1)

            def e_stats_of(k):
                after(dve, gathered[k.place], 16 * (k.turn + 1))
                nc.vector.bn_stats(e_st[:, :], edge_x[k.place]).then_inc(e_stats, 1)

            def e_moments_of(k):
                after_apart(dve, (e_stats, k.n + 1))
                nc.vector.bn_aggr(e_mv[k.place % 2][:, :], e_st[:, :]).then_inc(e_moments, 1)

            def e_variance(k):
                var = e_mv[k.place % 2][:, 1:2]
                after(dve, e_moments, k.n + 1)
                nc.vector.tensor_scalar(var, var, EPS, None, ALU.add).then_inc(e_var, 1)

            def e_scale_of(k):
                p = k.place % 2
                after(dve, e_rstd, k.n + 1)
                nc.vector.tensor_tensor(e_rv[p][:, :], e_rs[p][:, :], val[:, bass.ds(k.n, 1)],
                                        ALU.mult).then_inc(e_scale, 1)

            def same_target(k):
                after(dve, sumT_ps, k.n - 1)
                after(dve, src_row_ld[k.place], 16 * (k.turn + 1))
                nc.vector.tensor_scalar(same[k.place % 2][:, :], src_row[k.place][:, :],
                                        src_f[:, bass.ds(k.n, 1)], None, ALU.is_equal).then_inc(same_rdy, 1)

            def e_norm(k):
                p = k.place % 2
                after(dve, e_scale, k.n + 1)
                after(dve, edge_lo_rdy, k.n)
                nc.vector.tensor_scalar(edge_xn, edge_x[k.place], e_mv[p][:, 0:1], e_rv[p][:, :],
                                        ALU.subtract, ALU.mult).then_inc(edge_xn_rdy, 1)

            def count_earlier(k):
                after(dve, same_rdy, k.n + 1)
                nc.vector.tensor_tensor_reduce(out=same_before[:, :], in0=f32(same[k.place % 2][:, :]),
                                               in1=before[:, :], scale=1.0, scalar=0.0, op0=ALU.mult,
                                               op1=ALU.add, accum_out=earlier[:, :]).then_inc(earlier_rdy, 1)

            def target_shift(k):
                after(dve, earlier_rdy, k.n + 1)
                nc.vector.tensor_scalar(shift[:, :], earlier[:, :], 1.0, to_spare[:, bass.ds(k.n, 1)],
                                        ALU.min, ALU.mult).then_inc(shift_rdy, 1)

            def target_of(k):
                after(dve, shift_rdy, k.n + 1)
                nc.vector.tensor_tensor(target[:, bass.ds(k.n, 1)], src_f[:, bass.ds(k.n, 1)], shift[:, :],
                                        ALU.add).then_inc(target_rdy, 1)

            def edge_low(k):
                low_part(edge_lo[:, :], edge_xn, edge_hi[:, :], edge_hi_rdy, k.n + 1, edge_lo_rdy)

            def sumT_low(k):
                hi, lo = sumT[k.place % 2]
                low_part(lo[:, :, :], chunked(p_sumT[k.place % 2]), hi[:, :, :], sumT_hi, k.n + 1, sumT_lo)

            def edges(k):
                k1, k2, k4 = k.plus(1), k.plus(2), k.plus(4)
                has2, has4 = k2.within(EDGE_TILES), k4.within(EDGE_TILES)
                if has2:
                    e_scale_of(k2)
                    same_target(k2)
                    e_norm(k2)
                    count_earlier(k2)
                if has4:
                    e_stats_of(k4)
                if k1.within(EDGE_TILES):
                    sumT_low(k1)
                if has2:
                    target_shift(k2)
                    edge_low(k2)
                if has4:
                    e_moments_of(k4)
                if has2:
                    target_of(k2)
                if has4:
                    e_variance(k4)

            for k in range(2):
                e_stats_of(four(k))
                e_moments_of(four(k))
                e_variance(four(k))
            a_moments_of(pair(LEAD))
            a_norm(pair(LEAD))
            gate_bias(pair(LEAD - 1))
            edges(four(-2))
            trans_bias(pair(LEAD - 1))
            for k in range(-1, EDGE_SLOTS):
                edges(four(k))
            with dve.Fori(1, EDGE_TILES // EDGE_SLOTS - 1) as q:
                for place in range(EDGE_SLOTS):
                    edges(At(q, place, EDGE_SLOTS))
            for k in range(EDGE_TILES - EDGE_SLOTS, EDGE_TILES):
                edges(four(k))

            xnT_low(pair(LEAD))
            weight_lo(WW)
            weight_lo(WV)
            low_part(wg_parts[:, :, NE:], wg_raw[:, :, :], wg_parts[:, :, 0:NE], wg_hi, 1, wg_lo)

            def mix(u):
                after(dve, agg_ld[u.place], 16 * (u.turn + 1))
                trans = t_ring[:, u.n % LEAD, :]
                nc.vector.scalar_tensor_tensor(diff, agg_in[u.place], 0.0, trans, ALU.max,
                                               ALU.subtract).then_inc(diff_rdy, 1)
                after(dve, gate_tanh, u.n + 1)
                after(dve, diff_rdy, u.n + 1)
                nc.vector.scalar_tensor_tensor(diff, g_ring[:, u.n % LEAD, :], 1.0, diff, ALU.add,
                                               ALU.mult).then_inc(gated_rdy, 1)
                after(dve, gated_rdy, u.n + 1)
                nc.vector.scalar_tensor_tensor(mixed, diff, 0.5, trans, ALU.mult,
                                               ALU.add).then_inc(mixed_rdy, 1)

            def b_moments_of(u):
                after(dve, x1_rdy, u.n + 1)
                nc.vector.bn_stats(b_st[:, :], x_ring[:, u.n % X_RING, :]).then_inc(b_stats, 1)
                after_apart(dve, (b_stats, u.n + 1))
                nc.vector.bn_aggr(b_mv[:, :], b_st[:, :]).then_inc(b_moments, 1)

            def b_norm(u):
                after(dve, x1nT_ps, u.n)
                after(dve, b_rstd, u.n + 1)
                nc.vector.tensor_scalar(x1n, x_ring[:, u.n % X_RING, :], b_mv[:, 0:1], b_rs[:, :],
                                        ALU.subtract, ALU.mult).then_inc(x1n_rdy, 1)

            def x1nT_low(u):
                low_part(x1nT[1], chunked(p_x1nT), x1nT[0], x1nT_hi, u.n + 1, x1nT_lo)

            def hT_low(v):
                low_part(hT[1], chunked(p_xnT_hT), hT[0], hT_hi, v.n + 1, hT_lo)

            def activate(u):
                after(dve, h_rdy, u.n)
                after(dve, z_tanh_rdy, u.n + 1)
                nc.vector.scalar_tensor_tensor(act, z_tanh, 1.0, p_zw[:, :], ALU.add,
                                               ALU.mult).then_inc(silu_rdy, 1)

            def multiply(u):
                after(dve, zv_ps, u.n + 1)
                after(dve, silu_rdy, u.n + 1)
                nc.vector.tensor_tensor(act, act, p_zv[:, :], ALU.mult).then_inc(act_rdy, 1)

            def logits(u):
                after(dve, logit_ps, u.n + 1)
                nc.vector.tensor_copy(logit_parts[:, :], p_logit_rows).then_inc(logit_parts_rdy, 1)
                after(dve, logit_parts_rdy, u.n + 1)
                nc.vector.tensor_tensor(logit[:, :], logit_parts[:, 0:NE], logit_parts[:, NE:],
                                        ALU.add).then_inc(logit_rdy, 1)
                after_apart(dve, (logit_rdy, u.n + 1))
                nc.vector.max(best[:, :], logit[:, :]).then_inc(best_rdy, 1)
                after_apart(dve, (best_rdy, u.n + 1))
                nc.vector.max_index(best_i[:, :], best[:, :], logit[:, :]).then_inc(best_i_rdy, 1)
                nc.vector.tensor_tensor(gap[:, :], best[:, 1:2], best[:, 0:1], ALU.subtract).then_inc(gap_rdy, 1)
                after(dve, best_i_rdy, u.n + 1)
                nc.vector.tensor_copy(best_f[:, :], best_i[:, 0:2]).then_inc(best_f_rdy, 1)

            def shares(u):
                after(dve, e2_rdy, u.n + 1)
                nc.vector.tensor_scalar(total[:, :], e2[:, :], 1.0, 2.0, ALU.add, ALU.mult).then_inc(total_rdy, 1)
                after(dve, total_rdy, u.n + 1)
                nc.vector.reciprocal(share[:, 0:1], total[:, :]).then_inc(share1_rdy, 1)
                after(dve, share1_rdy, u.n + 1)
                nc.vector.tensor_tensor(share[:, 1:2], share[:, 0:1], e2[:, :], ALU.mult).then_inc(share2_rdy, 1)
                after(dve, best_f_rdy, u.n + 1)
                nc.vector.tensor_scalar(gw1[:, :], expert_f[:, :], best_f[:, 0:1], share[:, 0:1],
                                        ALU.is_equal, ALU.mult).then_inc(gw12_rdy, 1)
                after(dve, share2_rdy, u.n + 1)
                nc.vector.tensor_scalar(gw2[:, :], expert_f[:, :], best_f[:, 1:2], share[:, 1:2],
                                        ALU.is_equal, ALU.mult).then_inc(gw12_rdy, 1)
                after(dve, h_rdy, u.n)
                after(dve, gw12_rdy, 2 * u.n + 2)
                nc.vector.tensor_tensor(gw[:, :], gw1[:, :], gw2[:, :], ALU.add).then_inc(gw_rdy, 1)

            def residual(v):
                after(dve, out_st[v.place], 16 * v.turn)
                after(dve, y_ps, v.n + 1)
                nc.vector.tensor_tensor(out_sb[v.place], p_y[:, :], x_ring[:, v.n % X_RING, :],
                                        ALU.add).then_inc(out_rdy, 1)

            def rows(u):
                t = u.plus(LEAD)
                if not u.is_first():
                    xnT_low(t)
                activate(u)
                multiply(u)
                logits(u)
                x1nT_low(u.plus(1))
                shares(u)
                if not u.is_first():
                    residual(u.plus(-1))
                mix(u.plus(2))
                if t.plus(1).within(TILES):
                    a_moments_of(t.plus(1))
                gate_bias(t)
                if t.plus(1).within(TILES):
                    a_norm(t.plus(1))
                b_moments_of(u.plus(2))
                trans_bias(t)
                hT_low(u)
                b_norm(u.plus(2))

            def last_rows(u):
                if u.plus(2).within(TILES):
                    mix(u.plus(2))
                activate(u)
                logits(u)
                shares(u)
                multiply(u)
                if u.plus(1).within(TILES):
                    x1nT_low(u.plus(1))
                if u.plus(2).within(TILES):
                    b_moments_of(u.plus(2))
                residual(u.plus(-1))
                hT_low(u)
                if u.plus(2).within(TILES):
                    b_norm(u.plus(2))

            mix(pair(0))
            b_moments_of(pair(0))
            b_norm(pair(0))
            mix(pair(1))
            x1nT_low(pair(0))
            b_moments_of(pair(1))
            b_norm(pair(1))
            weight_lo(WO)
            for u in range(4):
                rows(pair(u))
            with dve.Fori(2, (TILES - LEAD) // 2 - 1) as i:
                rows(At(i, 0, 2))
                rows(At(i, 1, 2))
            for u in range(TILES - LEAD - 2, TILES - LEAD):
                rows(pair(u))
            for u in range(TILES - LEAD, TILES):
                last_rows(pair(u))
            residual(pair(TILES - 1))

        @block.tensor
        def _(pe):
            def product(ps, lhsT, rhs):
                terms = [(lhsT[a], rhs[b], c) for c in range(C) for a, b in ((0, 0), (0, 1), (1, 0))]
                for n, (a, b, c) in enumerate(terms):
                    last = nc.tensor.matmul(ps, a[:, c, :], b[:, c, :], start=n == 0, stop=n == len(terms) - 1)
                return last

            def transposed(ps, rows):
                for c in range(C):
                    last = nc.tensor.transpose(ps[:, c * P:(c + 1) * P], rows[:, c * P:(c + 1) * P], ident[:, :])
                return last

            def xn_transpose(t, v):
                if v is not None:
                    after(pe, hT_lo, v.n + 1)
                after(pe, xn_rdy, t.n + 1)
                transposed(p_xnT_hT, xn).then_inc(xnT_ps, 1)

            def gate_product(t):
                after(pe, gate_sb, t.n)
                after(pe, xnT_lo, t.n + 1)
                product(p_gate[:, :], xnT[t.place], w3p).then_inc(gate_ps, 1)

            def trans_product(t):
                after(pe, trans_sb, t.n)
                product(p_trans[:, :], xnT[t.place], w2p).then_inc(trans_ps, 1)

            pe.wait_ge(ident_rdy, 1)
            xn_transpose(pair(0), None)
            pe.wait_ge(w_lo, W3 + 1)

            def ahead(t):
                gate_product(t)
                if not (isinstance(t.n, int) and t.n == LEAD - 1):
                    xn_transpose(t.plus(1), None)
                trans_product(t)

            gate_product(pair(0))
            xn_transpose(pair(1), None)
            pe.wait_ge(w_lo, W2 + 1)
            trans_product(pair(0))
            ahead(pair(1))
            with pe.Fori(1, LEAD // 2) as i:
                ahead(At(i, 0, 2))
                ahead(At(i, 1, 2))
            ahead(pair(LEAD - 1))

            def sums(k):
                p = k.place % 2
                after(pe, edge_lo_rdy, k.n + 1)
                for c in range(C):
                    cols = slice(c * P, (c + 1) * P)
                    nc.tensor.matmul(p_sumT[p][:, cols], edge_hi[:, cols], same[p][:, :], start=True, stop=False)
                    last = nc.tensor.matmul(p_sumT[p][:, cols], edge_lo[:, cols], same[p][:, :],
                                            start=False, stop=True)
                last.then_inc(sumT_ps, 1)

            def messages(k):
                p = k.place % 2
                after(pe, msg_sb, k.n - 1)
                after(pe, sumT_lo, k.n + 1)
                product(p_msg[p][:, :], sumT[p], w1O).then_inc(msg_ps, 1)

            def edges(k):
                if k.plus(1).within(EDGE_TILES):
                    sums(k.plus(1))
                if k.within(EDGE_TILES):
                    messages(k)

            edges(four(-1))
            pe.wait_ge(w_lo, W1 + 1)
            for k in range(EDGE_SLOTS):
                edges(four(k))
            with pe.Fori(1, EDGE_TILES // EDGE_SLOTS - 1) as q:
                for place in range(EDGE_SLOTS):
                    edges(At(q, place, EDGE_SLOTS))
            for k in range(EDGE_TILES - EDGE_SLOTS, EDGE_TILES):
                edges(four(k))

            def x1n_transpose(u):
                after(pe, x1n_rdy, u.n + 1)
                transposed(p_x1nT, x1n).then_inc(x1nT_ps, 1)

            def logit_transpose(u):
                after_apart(pe, (logit_T_sb, u.n + 1))
                nc.tensor.transpose(p_logit_rows, logit_parts_T[:, :], ident[0:2 * NE, 0:2 * NE]).then_inc(logit_ps, 1)

            def experts_in(u):
                after(pe, x1nT_lo, u.n + 1)
                for c in range(C):
                    for part in range(2):
                        last = nc.tensor.matmul(p_logit_T, wg_parts[:, c, :], x1nT[part][:, c, :],
                                                start=c + part == 0, stop=c + part == C)
                last.then_inc(logit_T_ps, 1)
                product(p_zw[:, :], x1nT, wWp).then_inc(zw_ps, 1)
                if u.plus(LEAD).within(TILES):
                    product(p_zv[:, :], x1nT, wVp).then_inc(zv_ps, 1)
                    logit_transpose(u)
                else:
                    logit_transpose(u)
                    product(p_zv[:, :], x1nT, wVp).then_inc(zv_ps, 1)

            def h_transpose(u):
                after(pe, h_rdy, u.n + 1)
                transposed(p_xnT_hT, h).then_inc(hT_ps, 1)

            def experts_out(v):
                after(pe, out_rdy, v.n)
                if v.plus(LEAD + 1).beyond(TILES):
                    after(pe, hT_lo, v.n + 1)
                product(p_y[:, :], hT, w1O).then_inc(y_ps, 1)

            def rows(u):
                t = u.plus(LEAD)
                experts_in(u)
                if t.within(TILES) and not u.is_first():
                    xn_transpose(t, u.plus(-1))
                if u.plus(1).within(TILES):
                    x1n_transpose(u.plus(1))
                if u.plus(-1).within(TILES):
                    experts_out(u.plus(-1))
                if t.within(TILES) and not u.is_first():
                    gate_product(t)
                    trans_product(t)
                h_transpose(u)

            xn_transpose(pair(LEAD), None)
            gate_product(pair(LEAD))
            trans_product(pair(LEAD))
            x1n_transpose(pair(0))
            pe.wait_ge(wg_lo, 1)
            pe.wait_ge(w_lo, WV + 1)
            rows(pair(0))
            pe.wait_ge(w_lo, WO + 1)
            rows(pair(1))
            with pe.Fori(1, (TILES - LEAD) // 2 - 1) as i:
                rows(At(i, 0, 2))
                rows(At(i, 1, 2))
            for u in range(TILES - LEAD - 2, TILES):
                rows(pair(u))
            experts_out(pair(TILES - 1))


def kernel(x, src, dst, edge_weight, L0_gnn_w1, L0_gnn_w2, L0_gnn_w3, L0_gnn_b1, L0_gnn_b2, L0_gnn_b3,
           L0_ffn_Wg, L0_ffn_W, L0_ffn_V, L0_ffn_W2):
    import numpy as np
    import concourse.bacc as bacc
    from concourse.bass_utils import run_bass_kernel_spmd

    rows, d = x.shape
    padded = -(-rows // P) * P
    edge_rows = EDGE_SLOTS * P
    edges = -(-len(src) // edge_rows) * edge_rows
    if padded == rows:
        padded += P

    xp = np.zeros((padded, d), x.dtype)
    xp[:rows] = x
    srcp = np.full(edges, padded - 1, src.dtype)
    srcp[:len(src)] = src
    dstp = np.zeros(edges, dst.dtype)
    dstp[:len(dst)] = dst
    valp = np.zeros(edges, edge_weight.dtype)
    valp[:len(edge_weight)] = edge_weight

    def columns(a):
        return np.ascontiguousarray(np.asarray(a).reshape(-1, P).T)

    def experts_side_by_side(w):
        return np.ascontiguousarray(np.transpose(np.asarray(w), (1, 0, 2)).reshape(d, -1))

    arrays = {
        "x": xp, "src_rows": srcp, "src_cols": columns(srcp), "dst_cols": columns(dstp),
        "val_cols": columns(valp), "w1": L0_gnn_w1, "w2": L0_gnn_w2, "w3": L0_gnn_w3,
        "b1": L0_gnn_b1, "b2": L0_gnn_b2, "b3": L0_gnn_b3, "wg": L0_ffn_Wg,
        "wW": experts_side_by_side(L0_ffn_W), "wV": experts_side_by_side(L0_ffn_V),
        "wO": np.asarray(L0_ffn_W2).reshape(-1, d),
    }
    arrays = {k: np.ascontiguousarray(v) for k, v in arrays.items()}
    nc = bacc.Bacc("TRN2", target_bir_lowering=False, num_devices=1)
    ins = {k: nc.dram_tensor("in_" + k, v.shape, mybir.dt.from_np(v.dtype), kind="ExternalInput").ap()
           for k, v in arrays.items()}
    out = nc.dram_tensor("out_rows", (padded, d), F32, kind="ExternalOutput").ap()
    gnn_experts_kernel(nc, **ins, out=out)
    r = run_bass_kernel_spmd(nc, [{"in_" + k: v for k, v in arrays.items()}], core_ids=[0])
    return r.results[0]["out_rows"][:rows]
```

```python
from contextlib import ExitStack

import concourse.bass as bass
from concourse import mybir

F32 = mybir.dt.float32
F32R = mybir.dt.float32r
I32 = mybir.dt.int32
U32 = mybir.dt.uint32
ALU = mybir.AluOpType
ACT = mybir.ActivationFunctionType

P = 128
LEAD = 9
EPS = 1e-5
EDGE_SLOTS = 4
AHEAD_FILLS = 3
EARLY = 2


class At:

    def __init__(self, turn, place, unroll):
        self.turn, self.place, self.unroll = turn, place, unroll
        self.n = turn * unroll + place

    def plus(self, k):
        turns, place = divmod(self.place + k, self.unroll)
        return At(self.turn + turns, place, self.unroll)

    def within(self, count):
        return not isinstance(self.n, int) or 0 <= self.n < count

    def beyond(self, count):
        return isinstance(self.n, int) and self.n >= count

    def below(self, count):
        return isinstance(self.n, int) and self.n < count


def pair(n):
    return At(n // 2, n % 2, 2)


def four(n):
    return At(n // EDGE_SLOTS, n % EDGE_SLOTS, EDGE_SLOTS)


def after(eng, sem, count):
    if not isinstance(count, int) or count > 0:
        eng.wait_ge(sem, count)


def after_apart(eng, *waits):
    if isinstance(waits[0][1], int):
        for sem, count in waits:
            after(eng, sem, count)
        return
    counts = [eng.snap(count) for _, count in waits]
    for count in counts:
        eng.compute_val(count)
    eng.wait_ge(waits[0][0], 1)
    for (sem, _), count in zip(waits, counts):
        eng.wait_ge(sem, count)


def gnn_experts_kernel(nc, x, xT, src_rows, src_cols, dst_cols, val_cols, w1, w2, w3, b1, b2, b3,
                       wg, wW, wV, wO, out):
    ROWS, D = x.shape
    TILES = ROWS // P
    C = D // P
    EDGE_TILES = src_cols.shape[1]
    NE = wg.shape[1]
    FE = D // NE
    SPARE = ROWS
    X_RING = LEAD + 4
    FILL_ROWS = 512
    FILLS = (ROWS + P) // FILL_ROWS
    assert D == 512 and ROWS % P == 0 and (TILES - LEAD) % 2 == 0 and LEAD % 2 == 1
    assert EDGE_TILES % EDGE_SLOTS == 0 and 2 * C % EDGE_SLOTS == 0 and EDGE_TILES >= 5 * NE and (ROWS + P) % FILL_ROWS == 0 and FILLS >= 2 * LEAD + 2

    agg = nc.dram_tensor("agg", (ROWS + P, D), F32, kind="Internal").ap()

    with ExitStack() as ctx:
        def sb(name, shape, dt=F32):
            return ctx.enter_context(nc.sbuf_tensor(name, shape, dt))

        def sem(name):
            return ctx.enter_context(nc.semaphore(name))

        ident = sb("ident", [P, P])
        before = sb("before", [P, P])
        minus_half = sb("minus_half", [P, 1])
        expert_i = sb("expert_i", [P, NE], I32)
        expert_f = sb("expert_f", [P, NE])
        spare_i = sb("spare_i", [P, 1], I32)
        spare_f = sb("spare_f", [P, 1])
        b2_all = sb("b2_all", [P, D])
        b3_all = sb("b3_all", [P, D])

        stage = [sb(f"stage{i}", [P, C, D]) for i in range(2)]
        def parts(name, n=D):
            return sb(name + "_hi", [P, C, n], F32R), sb(name + "_lo", [P, C, n], F32R)
        w1O = parts("w1_then_wO")
        w2p, w3p, wWp, wVp = parts("w2"), parts("w3"), parts("wW"), parts("wV")
        wg_parts = sb("wg_parts", [P, C, 2 * NE], F32R)
        wg_raw = sb("wg_raw", [P, C, NE])
        weights = [(w3, w3p), (w2, w2p), (w1, w1O), (wW, wWp), (wV, wVp), (wO, w1O)]
        W3, W2, W1, WW, WV, WO = range(len(weights))
        CENTRED = 2

        x_ring = sb("x_ring", [P, X_RING, D])
        t_ring = sb("t_ring", [P, LEAD, D])
        g_ring = sb("g_ring", [P, LEAD, D])
        xT_in = [sb(f"xT_in{i}", [P, C, P]) for i in range(2)]
        xT_parts = [(sb(f"xT_hi{i}", [P, C, P], F32R), sb(f"xT_lo{i}", [P, C, P], F32R)) for i in range(2)]
        a_st = sb("a_st", [P, 6])
        a_mv = sb("a_mv", [P, 2])
        a_rs = [sb(f"a_rs{i}", [P, 1]) for i in range(2)]

        work = sb("work", [P, 10, D])
        edge_x = [work[:, i, :] for i in range(4)]
        edge_xn = work[:, 4, :]
        edge_msg = [work[:, 5 + i, :] for i in range(4)]
        b1_all = work[:, 9, :]
        pair_sum, chunk_sum, one_over_D = work[:, 4:6, :], work[:, 6, :], work[:, 7, 0:P]
        agg_in = [work[:, i, :] for i in range(2)]
        diff, mixed, x1n, z_tanh, act, h = (work[:, 2 + i, :] for i in range(6))
        out_sb = [work[:, 8 + i, :] for i in range(2)]

        workr = [sb(f"workr{i}", [P, D], F32R) for i in range(4)]
        edge_hi, edge_lo = workr[0], workr[1]
        def chunked(a):
            return a[:, :].rearrange("p (c m) -> p c m", c=C)
        x1nT = (chunked(workr[0]), chunked(workr[1]))
        hT = (chunked(workr[2]), chunked(workr[3]))
        sumT = xT_parts

        same = [workr[2][:, i * P:(i + 1) * P] for i in range(2)]
        same_before = sb("same_before", [P, P])
        src_row = [sb(f"src_row{i}", [P, P], I32) for i in range(4)]
        src_i = sb("src_i", [P, EDGE_TILES], I32)
        dst_i = sb("dst_i", [P, EDGE_TILES], I32)
        val = sb("val", [P, EDGE_TILES])
        src_f = sb("src_f", [P, EDGE_TILES])
        to_spare = sb("to_spare", [P, EDGE_TILES])
        target = src_i
        dst_idx = [sb(f"dst_idx{i}", [P, 1], I32) for i in range(4)]
        src_idx = [sb(f"src_idx{i}", [P, 1], I32) for i in range(4)]
        earlier = sb("earlier", [P, 1])
        shift = sb("shift", [P, 1])
        e_st = sb("e_st", [P, 6])
        e_mv = [sb(f"e_mv{i}", [P, 2]) for i in range(2)]
        e_rs = [sb(f"e_rs{i}", [P, 1]) for i in range(2)]
        e_rv = [sb(f"e_rv{i}", [P, 1]) for i in range(2)]

        b_st = sb("b_st", [P, 6])
        b_mv = sb("b_mv", [P, 2])
        b_rs = sb("b_rs", [P, 1])
        logit_parts_T = same_before[0:2 * NE, :]
        logit_parts, gw1, gw2, gw = (val[:, i * NE:j * NE] for i, j in ((0, 2), (2, 3), (3, 4), (4, 5)))
        logit = sb("logit", [P, NE])
        best = sb("best", [P, 8])
        best_i = sb("best_i", [P, 8], U32)
        best_f = sb("best_f", [P, 2])
        gap = sb("gap", [P, 1])
        e2 = sb("e2", [P, 1])
        total = sb("total", [P, 1])
        share = sb("share", [P, 2])

        bank = [ctx.enter_context(nc.psum_tensor(f"bank{i}", [P, D], F32)) for i in range(8)]
        p_hT, p_x1nT, p_gate, p_trans, p_zw, p_zv, p_y, p_logit = bank
        p_sumT = [p_zw, p_zv]
        p_msg = [p_y, p_logit]
        p_logit_T = p_logit[0:2 * NE, 0:P]
        p_mean = [p_gate, p_trans]
        p_logit_rows = p_logit[:, P:P + 2 * NE]

        consts_ld = sem("consts_ld")
        edges_ld = sem("edges_ld")
        b1_ld = sem("b1_ld")
        filled = [sem(f"filled{i}") for i in range(2)]
        stage_ld = [sem(f"stage_ld{i}") for i in range(2)]
        wg_ld = sem("wg_ld")
        w_hi = sem("w_hi")
        w_lo = sem("w_lo")
        wg_hi = sem("wg_hi")
        wg_lo = sem("wg_lo")
        memset_done = sem("memset_done")
        ident_rdy = sem("ident_rdy")
        before_rdy = sem("before_rdy")
        iota_rdy = sem("iota_rdy")
        spare_rdy = sem("spare_rdy")
        expert_rdy = sem("expert_rdy")
        src_f_rdy = sem("src_f_rdy")
        to_spare_rdy = sem("to_spare_rdy")

        w_sum = sem("w_sum")
        w_pairs = sem("w_pairs")
        w_mean = sem("w_mean")
        w_centred = sem("w_centred")

        x_ld = [sem(f"x_ld{i}") for i in range(2)]
        xT_ld = [sem(f"xT_ld{i}") for i in range(2)]
        a_stats = sem("a_stats")
        a_moments = sem("a_moments")
        a_var = sem("a_var")
        a_rstd = sem("a_rstd")
        xT_hi = sem("xT_hi")
        xT_lo = sem("xT_lo")
        gate_ps = sem("gate_ps")
        trans_ps = sem("trans_ps")
        gate_sb = sem("gate_sb")
        gate_tanh = sem("gate_tanh")
        trans_sb = sem("trans_sb")

        src_row_ld = [sem(f"src_row_ld{i}") for i in range(4)]
        dst_idx_rdy = sem("dst_idx_rdy")
        gathered = [sem(f"gathered{i}") for i in range(4)]
        same_rdy = sem("same_rdy")
        earlier_rdy = sem("earlier_rdy")
        shift_rdy = sem("shift_rdy")
        target_rdy = sem("target_rdy")
        e_stats = sem("e_stats")
        e_moments = sem("e_moments")
        e_var = sem("e_var")
        e_rstd = sem("e_rstd")
        e_scale = sem("e_scale")
        edge_xn_rdy = sem("edge_xn_rdy")
        edge_hi_rdy = sem("edge_hi_rdy")
        edge_lo_rdy = sem("edge_lo_rdy")
        sumT_ps = sem("sumT_ps")
        sumT_hi = sem("sumT_hi")
        sumT_lo = sem("sumT_lo")
        msg_ps = sem("msg_ps")
        msg_sb = sem("msg_sb")
        src_idx_rdy = sem("src_idx_rdy")
        added = sem("added")

        agg_ld = [sem(f"agg_ld{i}") for i in range(2)]
        diff_rdy = sem("diff_rdy")
        gated_rdy = sem("gated_rdy")
        mixed_rdy = sem("mixed_rdy")
        x1_rdy = sem("x1_rdy")
        b_stats = sem("b_stats")
        b_moments = sem("b_moments")
        b_var = sem("b_var")
        b_rstd = sem("b_rstd")
        x1n_rdy = sem("x1n_rdy")
        x1nT_ps = sem("x1nT_ps")
        x1nT_hi = sem("x1nT_hi")
        x1nT_lo = sem("x1nT_lo")
        zw_ps = sem("zw_ps")
        zv_ps = sem("zv_ps")
        z_tanh_rdy = sem("z_tanh_rdy")
        silu_rdy = sem("silu_rdy")
        act_rdy = sem("act_rdy")
        logit_T_ps = sem("logit_T_ps")
        logit_T_sb = sem("logit_T_sb")
        logit_ps = sem("logit_ps")
        logit_parts_rdy = sem("logit_parts_rdy")
        logit_rdy = sem("logit_rdy")
        best_rdy = sem("best_rdy")
        best_i_rdy = sem("best_i_rdy")
        gap_rdy = sem("gap_rdy")
        best_f_rdy = sem("best_f_rdy")
        e2_rdy = sem("e2_rdy")
        total_rdy = sem("total_rdy")
        share1_rdy = sem("share1_rdy")
        share2_rdy = sem("share2_rdy")
        gw12_rdy = sem("gw12_rdy")
        gw_rdy = sem("gw_rdy")
        h_rdy = sem("h_rdy")
        hT_ps = sem("hT_ps")
        hT_hi = sem("hT_hi")
        hT_lo = sem("hT_lo")
        y_ps = sem("y_ps")
        out_rdy = sem("out_rdy")
        out_st = [sem(f"out_st{i}") for i in range(2)]

        block = ctx.enter_context(nc.Block())

        @block.sync
        def _(sp):
            def load_weight_chunk(i, c):
                sp.dma_start(stage[i % 2][:, c, :], weights[i][0][c * P:(c + 1) * P, :]).then_inc(stage_ld[i % 2], 16)

            def load_weight(i):
                after(sp, w_lo, i - 1)
                for c in range(C):
                    load_weight_chunk(i, c)

            def load_x(t):
                sp.dma_start(x_ring[:, t.n % X_RING, :], x[bass.ds(t.n * P, P), :]).then_inc(x_ld[t.place], 16)

            def load_xT(t):
                after(sp, xT_lo, t.n - 1)
                sp.dma_start(xT_in[t.place][:, :, :], xT[bass.ds(t.n * P, P), :].rearrange("p (c r) -> p c r", c=C)
                             ).then_inc(xT_ld[t.place], 16)

            def fill(i):
                after(sp, filled[i % 2], 16 * (i // 2))
                sp.dma_start(agg[i * FILL_ROWS:(i + 1) * FILL_ROWS, :].rearrange("(a p) d -> p a d", p=P),
                             b1_all.unsqueeze(1).to_broadcast([P, FILL_ROWS // P, D])).then_inc(filled[i % 2], 16)

            def load_src_row(k):
                after(sp, same_rdy, k.n - EDGE_SLOTS + 1)
                sp.dma_start(src_row[k.place][:, :],
                             src_rows[bass.ds(k.n * P, P)].partition_broadcast(P)).then_inc(src_row_ld[k.place], 16)

            def load_agg(u):
                sp.dma_start(agg_in[u.place], agg[bass.ds(u.n * P, P), :]).then_inc(agg_ld[u.place], 16)

            load_weight(W3)
            load_x(pair(0))
            load_xT(pair(0))
            sp.dma_start(b1_all, b1.partition_broadcast(P)).then_inc(b1_ld, 16)
            load_weight(W2)
            load_x(pair(1))
            load_xT(pair(1))
            sp.dma_start(b3_all[:, :], b3.partition_broadcast(P)).then_inc(consts_ld, 16)
            sp.dma_start(b2_all[:, :], b2.partition_broadcast(P)).then_inc(consts_ld, 16)
            for edge_in, at in ((src_i, src_cols), (dst_i, dst_cols), (val, val_cols)):
                sp.dma_start(edge_in[:, :], at).then_inc(edges_ld, 16)
            sp.wait_ge(b1_ld, 16)
            for i in range(AHEAD_FILLS):
                fill(i)
            for t in range(LEAD):
                after(sp, a_stats, t + 1)
                if t + 2 < LEAD:
                    load_x(pair(t + 2))
                    load_xT(pair(t + 2))
                if t == 2:
                    load_weight(W1)
                if t == 3:
                    for k in range(EDGE_SLOTS):
                        load_src_row(four(k))
                fill(t + AHEAD_FILLS)
            for i in range(LEAD + AHEAD_FILLS, FILLS):
                if i >= FILLS - EDGE_SLOTS + 1:
                    load_src_row(four(EDGE_SLOTS + i - (FILLS - EDGE_SLOTS + 1)))
                fill(i)
            load_src_row(four(2 * EDGE_SLOTS - 1))
            for k in range(EDGE_SLOTS):
                load_src_row(four(2 * EDGE_SLOTS + k))
                (load_x, load_xT)[k % 2](pair(LEAD + k // 2))
            sp.dma_start(wg_raw[:, :, :], wg.rearrange("(c p) n -> p c n", p=P)).then_inc(wg_ld, 16)
            sp.wait_ge(w_lo, WV - 1)
            for k in range(2 * C):
                load_src_row(four(3 * EDGE_SLOTS + k))
                load_weight_chunk(WW + k // C, k % C)
            with sp.Fori(3 + 2 * C // EDGE_SLOTS, EDGE_TILES // EDGE_SLOTS) as q:
                for place in range(EDGE_SLOTS):
                    load_src_row(At(q, place, EDGE_SLOTS))

            sp.wait_ge(added, 16 * EDGE_TILES)
            load_agg(pair(0))
            load_agg(pair(1))
            load_weight(WO)
            sp.wait_ge(mixed_rdy, 1)
            load_agg(pair(2))

            def rows(u):
                t = u.plus(LEAD)
                if u.plus(3).within(TILES):
                    after(sp, mixed_rdy, u.n + 2)
                    load_agg(u.plus(3))
                if t.plus(2).within(TILES):
                    after_apart(sp, (a_stats, t.n + 1), (out_rdy, u.n - 1))
                    load_x(t.plus(2))
                    load_xT(t.plus(2))
                if u.plus(-1).within(TILES):
                    store_out(u.plus(-1))

            def store_out(v):
                after(sp, out_rdy, v.n + 1)
                sp.dma_start(out[bass.ds(v.n * P, P), :], out_sb[v.place]).then_inc(out_st[v.place], 16)

            rows(pair(0))
            rows(pair(1))
            with sp.Fori(1, (TILES - LEAD) // 2 - 1) as i:
                rows(At(i, 0, 2))
                rows(At(i, 1, 2))
            for u in range(TILES - LEAD - 2, TILES):
                rows(pair(u))
            store_out(pair(TILES - 1))
            for place in range(2):
                sp.wait_ge(out_st[place], 16 * ((TILES + 1 - place) // 2))

        @block.gpsimd
        def _(pool):
            nc.gpsimd.memset(one_over_D, 1.0 / D).then_inc(memset_done, 1)
            nc.gpsimd.memset(ident[:, :], 0.0).then_inc(memset_done, 1)
            nc.gpsimd.memset(before[:, :], 1.0).then_inc(memset_done, 1)
            nc.gpsimd.iota(expert_i[:, :], pattern=[[1, NE]], base=0, channel_multiplier=0).then_inc(iota_rdy, 1)
            nc.gpsimd.iota(spare_i[:, :], pattern=[[1, 1]], base=SPARE, channel_multiplier=1).then_inc(iota_rdy, 1)
            nc.gpsimd.memset(minus_half[:, :], -0.5).then_inc(memset_done, 1)
            pool.wait_ge(memset_done, 4)
            nc.gpsimd.affine_select(out=ident[:, :], in_=ident[:, :], compare_op=ALU.not_equal, fill=1.0,
                                    base=0, pattern=[[-1, P]], channel_multiplier=1).then_inc(ident_rdy, 1)
            nc.gpsimd.affine_select(out=before[:, :], in_=before[:, :], compare_op=ALU.is_gt, fill=0.0,
                                    base=0, pattern=[[-1, P]], channel_multiplier=1).then_inc(before_rdy, 1)

            def rstd(mv, rs, moments, n, var_rdy, done):
                after_apart(pool, (moments, n + 1))
                nc.gpsimd.tensor_scalar(rs[:, :], mv[:, 1:2], EPS, None, ALU.add).then_inc(var_rdy, 1)
                after(pool, var_rdy, n + 1)
                nc.gpsimd.tensor_tensor(rs[:, :], rs[:, :], minus_half[:, :], ALU.pow).then_inc(done, 1)

            def gather(k):
                after_apart(pool, (dst_idx_rdy, k.n + 1), (edge_xn_rdy, k.n - EDGE_SLOTS + 1))
                pool.indirect_dma_start(
                    out=edge_x[k.place], out_offset=None, in_=x,
                    in_offset=bass.IndirectOffsetOnAxis(ap=dst_idx[k.place][:, 0:1], axis=0),
                ).then_inc(gathered[k.place], 16)

            def a_rstd_of(t):
                rstd(a_mv, a_rs[t.place], a_moments, t.n, a_var, a_rstd)

            a_rstd_of(pair(0))
            a_rstd_of(pair(1))
            for k in range(EDGE_SLOTS):
                gather(four(k))
                a_rstd_of(pair(k + 2))
            for t in range(EDGE_SLOTS + 2, LEAD):
                a_rstd_of(pair(t))


            def edge_rstd(k):
                p = k.place % 2
                after(pool, e_var, k.n + 1)
                nc.gpsimd.tensor_tensor(e_rs[p][:, :], e_mv[p][:, 1:2], minus_half[:, :],
                                        ALU.pow).then_inc(e_rstd, 1)

            def edges(k):
                if k.plus(7).within(EDGE_TILES) and not k.below(EARLY):
                    gather(k.plus(7))
                if k.plus(5).within(EDGE_TILES) and not k.below(EARLY):
                    edge_rstd(k.plus(5))
                if k.below(1):
                    for i in range(2):
                        pool.wait_ge(filled[i], 16 * ((FILLS + 1 - i) // 2))
                after_apart(pool, (src_idx_rdy, k.n + 1), (msg_sb, k.n + 1), (added, k.n * 16))
                pool.indirect_dma_start(
                    out=agg, out_offset=bass.IndirectOffsetOnAxis(ap=src_idx[k.place][:, 0:1], axis=0),
                    in_=edge_msg[k.place], in_offset=None, bounds_check=ROWS + P - 1, compute_op=ALU.add,
                ).then_inc(added, 16)

            for k in range(5 + EARLY):
                edge_rstd(four(k))
                if k >= 2:
                    gather(four(k + 2))
            for k in range(EDGE_SLOTS):
                edges(four(k))
            a_rstd_of(pair(LEAD))
            with pool.Fori(1, EDGE_TILES // EDGE_SLOTS - 2) as q:
                for place in range(EDGE_SLOTS):
                    edges(At(q, place, EDGE_SLOTS))
            for k in range(EDGE_TILES - 2 * EDGE_SLOTS, EDGE_TILES):
                edges(four(k))

            def x1(u):
                after(pool, mixed_rdy, u.n + 1)
                ring = x_ring[:, u.n % X_RING, :]
                nc.gpsimd.tensor_tensor(ring, mixed, ring, ALU.add).then_inc(x1_rdy, 1)

            def rows(u):
                t = u.plus(LEAD)
                if t.beyond(TILES) and u.plus(2).within(TILES):
                    x1(u.plus(2))
                after(pool, hT_ps, u.n)
                after(pool, act_rdy, u.n + 1)
                after(pool, gw_rdy, u.n + 1)
                nc.gpsimd.tensor_tensor(
                    h.rearrange("p (e f) -> p e f", e=NE), act.rearrange("p (e f) -> p e f", e=NE),
                    gw[:, :].unsqueeze(2).to_broadcast([P, NE, FE]), ALU.mult).then_inc(h_rdy, 1)
                if t.within(TILES):
                    x1(u.plus(2))
                if t.plus(1).within(TILES) and not u.below(1):
                    a_rstd_of(t.plus(1))
                if u.plus(2).within(TILES):
                    rstd(b_mv, b_rs, b_moments, u.n + 2, b_var, b_rstd)

            a_rstd_of(pair(LEAD + 1))
            for u in range(2):
                x1(pair(u))
                rstd(b_mv, b_rs, b_moments, u, b_var, b_rstd)
            rows(pair(0))
            rows(pair(1))
            with pool.Fori(1, (TILES - LEAD) // 2 - 1) as i:
                rows(At(i, 0, 2))
                rows(At(i, 1, 2))
            for u in range(TILES - LEAD - 2, TILES):
                rows(pair(u))

        @block.scalar
        def _(act_e):
            def weight_hi(i):
                if i < CENTRED:
                    act_e.wait_ge(w_centred, i + 1)
                else:
                    act_e.wait_ge(stage_ld[i % 2], 16 * C * (i // 2 + 1))
                nc.scalar.activation(weights[i][1][0][:, :, :], stage[i % 2][:, :, :], ACT.Copy).then_inc(w_hi, 1)

            def xT_high(t):
                after(act_e, trans_ps, t.n - 1)
                after(act_e, xT_ld[t.place], 16 * (t.turn + 1))
                nc.scalar.activation(xT_parts[t.place][0][:, :, :], xT_in[t.place][:, :, :],
                                     ACT.Copy).then_inc(xT_hi, 1)

            def gate_act(t):
                after(act_e, gate_sb, t.n + 1)
                ring = g_ring[:, t.n % LEAD, :]
                nc.scalar.activation(ring, ring, ACT.Tanh, scale=0.5).then_inc(gate_tanh, 1)

            def gather_index(k):
                after(act_e, gathered[k.place], 16 * k.turn)
                nc.scalar.activation(dst_idx[k.place][:, :], dst_i[:, bass.ds(k.n, 1)],
                                     ACT.Copy).then_inc(dst_idx_rdy, 1)

            xT_high(pair(0))
            weight_hi(W3)
            weight_hi(W2)

            def ahead(t):
                xT_high(t.plus(1))
                gate_act(t)

            ahead(pair(0))
            ahead(pair(1))
            act_e.wait_ge(edges_ld, 48)
            for k in range(EDGE_SLOTS):
                gather_index(four(k))
            with act_e.Fori(1, LEAD // 2) as i:
                ahead(At(i, 0, 2))
                ahead(At(i, 1, 2))
            weight_hi(W1)
            gate_act(pair(LEAD - 1))

            def edge_high(k):
                after(act_e, edge_xn_rdy, k.n + 1)
                after(act_e, sumT_ps, k.n)
                nc.scalar.activation(edge_hi[:, :], edge_xn, ACT.Copy).then_inc(edge_hi_rdy, 1)

            def sumT_high(k):
                after(act_e, sumT_ps, k.n + 1)
                after(act_e, msg_ps, k.n - 1)
                nc.scalar.activation(sumT[k.place % 2][0][:, :, :], chunked(p_sumT[k.place % 2]),
                                     ACT.Copy).then_inc(sumT_hi, 1)

            def message(k):
                after(act_e, added, (k.n - EDGE_SLOTS + 1) * 16)
                after(act_e, target_rdy, k.n + 1)
                nc.scalar.activation(src_idx[k.place][:, :], target[:, bass.ds(k.n, 1)],
                                     ACT.Copy).then_inc(src_idx_rdy, 1)
                after(act_e, msg_ps, k.n + 1)
                nc.scalar.activation(edge_msg[k.place], p_msg[k.place % 2][:, :], ACT.Copy).then_inc(msg_sb, 1)

            def edges(k):
                if k.plus(1).within(EDGE_TILES):
                    sumT_high(k.plus(1))
                if k.plus(2).within(EDGE_TILES):
                    edge_high(k.plus(2))
                if k.plus(6).within(EDGE_TILES):
                    gather_index(k.plus(6))
                if k.within(EDGE_TILES):
                    message(k)

            for k in range(-2, EDGE_SLOTS):
                edges(four(k))
            with act_e.Fori(1, EDGE_TILES // EDGE_SLOTS - 2) as q:
                for place in range(EDGE_SLOTS):
                    edges(At(q, place, EDGE_SLOTS))
            for k in range(EDGE_TILES - 2 * EDGE_SLOTS, EDGE_TILES):
                edges(four(k))

            act_e.wait_ge(msg_ps, EDGE_TILES)
            xT_high(pair(LEAD))
            xT_high(pair(LEAD + 1))
            weight_hi(WW)
            weight_hi(WV)
            act_e.wait_ge(wg_ld, 16)
            nc.scalar.activation(wg_parts[:, :, 0:NE], wg_raw[:, :, :], ACT.Copy).then_inc(wg_hi, 1)
            def x1nT_high(u):
                after(act_e, x1nT_ps, u.n + 1)
                nc.scalar.activation(x1nT[0], chunked(p_x1nT), ACT.Copy).then_inc(x1nT_hi, 1)

            def second_share(u):
                after(act_e, gap_rdy, u.n + 1)
                nc.scalar.activation(e2[:, :], gap[:, :], ACT.Exp).then_inc(e2_rdy, 1)

            def hT_high(v):
                after(act_e, hT_ps, v.n + 1)
                nc.scalar.activation(hT[0], chunked(p_hT), ACT.Copy).then_inc(hT_hi, 1)

            def rows(u):
                t = u.plus(LEAD)
                if u.plus(-1).within(TILES):
                    hT_high(u.plus(-1))
                after(act_e, logit_T_ps, u.n + 1)
                nc.scalar.activation(logit_parts_T[:, :], p_logit_T, ACT.Copy).then_inc(logit_T_sb, 1)
                after(act_e, silu_rdy, u.n)
                after(act_e, zw_ps, u.n + 1)
                nc.scalar.activation(z_tanh, p_zw[:, :], ACT.Tanh, scale=0.5).then_inc(z_tanh_rdy, 1)
                if t.beyond(TILES):
                    second_share(u)
                if t.within(TILES) and not u.below(2):
                    xT_high(t)
                if u.plus(1).within(TILES):
                    x1nT_high(u.plus(1))
                if t.within(TILES):
                    second_share(u)
                if t.within(TILES):
                    gate_act(t)

            x1nT_high(pair(0))
            weight_hi(WO)
            rows(pair(0))
            rows(pair(1))
            with act_e.Fori(1, (TILES - LEAD) // 2 - 1) as i:
                rows(At(i, 0, 2))
                rows(At(i, 1, 2))
            for u in range(TILES - LEAD - 2, TILES):
                rows(pair(u))
            hT_high(pair(TILES - 1))

        @block.vector
        def _(dve):
            def f32(a):
                return a.bitcast(F32)

            def low_part(out, whole, high, have_high, count, done):
                after(dve, have_high, count)
                nc.vector.tensor_tensor(out, whole, f32(high), ALU.subtract).then_inc(done, 1)

            def weight_lo(i):
                hi, lo = weights[i][1]
                low_part(lo[:, :, :], stage[i % 2][:, :, :], hi[:, :, :], w_hi, i + 1, w_lo)

            def a_moments_of(t):
                after(dve, x_ld[t.place], 16 * (t.turn + 1))
                nc.vector.bn_stats(a_st[:, :], x_ring[:, t.n % X_RING, :]).then_inc(a_stats, 1)
                after_apart(dve, (a_stats, t.n + 1))
                nc.vector.bn_aggr(a_mv[:, :], a_st[:, :]).then_inc(a_moments, 1)

            def xT_low(t):
                hi, lo = xT_parts[t.place]
                low_part(lo[:, :, :], xT_in[t.place][:, :, :], hi[:, :, :], xT_hi, t.n + 1, xT_lo)

            def gate_bias(t, bank=p_gate):
                after(dve, gate_ps, t.n + 1)
                after(dve, a_rstd, t.n + 1)
                nc.vector.scalar_tensor_tensor(g_ring[:, t.n % LEAD, :], bank[:, :], a_rs[t.place][:, :],
                                               b3_all[:, :], ALU.mult, ALU.add).then_inc(gate_sb, 1)

            def trans_bias(t):
                after(dve, trans_ps, t.n + 1)
                nc.vector.scalar_tensor_tensor(t_ring[:, t.n % LEAD, :], p_trans[:, :], a_rs[t.place][:, :],
                                               b2_all[:, :], ALU.mult, ALU.add).then_inc(trans_sb, 1)

            def chunks_added(i):
                dve.wait_ge(stage_ld[i], 16 * C)
                w = stage[i]
                nc.vector.tensor_tensor(pair_sum, w[:, 0:2, :], w[:, 2:4, :], ALU.add).then_inc(w_pairs, 1)
                dve.wait_ge(w_pairs, i + 1)
                after(dve, w_mean, i)
                nc.vector.tensor_tensor(chunk_sum, pair_sum[:, 0, :], pair_sum[:, 1, :], ALU.add).then_inc(w_sum, 1)

            def centred(i):
                dve.wait_ge(w_mean, i + 1)
                nc.vector.tensor_tensor(stage[i][:, :, :], stage[i][:, :, :],
                                        p_mean[i][:, :].unsqueeze(1).to_broadcast([P, C, D]),
                                        ALU.subtract).then_inc(w_centred, 1)

            chunks_added(W3)
            centred(W3)
            a_moments_of(pair(0))
            chunks_added(W2)
            weight_lo(W3)
            xT_low(pair(0))
            centred(W2)
            dve.wait_ge(a_var, 1)
            a_moments_of(pair(1))
            weight_lo(W2)
            dve.wait_ge(consts_ld, 32)

            def ahead(t):
                xT_low(t.plus(1))
                gate_bias(t)
                a_moments_of(t.plus(1))
                trans_bias(t)

            xT_low(pair(1))
            gate_bias(pair(0))
            trans_bias(pair(0))
            ahead(pair(1))
            with dve.Fori(1, LEAD // 2) as i:
                ahead(At(i, 0, 2))
                ahead(At(i, 1, 2))

            dve.wait_ge(iota_rdy, 2)
            nc.vector.tensor_copy(spare_f[:, :], spare_i[:, :]).then_inc(spare_rdy, 1)
            nc.vector.tensor_copy(expert_f[:, :], expert_i[:, :]).then_inc(expert_rdy, 1)
            dve.wait_ge(edges_ld, 48)
            nc.vector.tensor_copy(src_f[:, :], src_i[:, :]).then_inc(src_f_rdy, 1)
            dve.wait_ge(spare_rdy, 1)
            dve.wait_ge(src_f_rdy, 1)
            nc.vector.tensor_scalar(to_spare[:, :], src_f[:, :], -1.0, spare_f[:, :],
                                    ALU.mult, ALU.add).then_inc(to_spare_rdy, 1)
            dve.wait_ge(to_spare_rdy, 1)
            dve.wait_ge(before_rdy, 1)
            weight_lo(W1)

            def e_stats_of(k):
                after(dve, gathered[k.place], 16 * (k.turn + 1))
                nc.vector.bn_stats(e_st[:, :], edge_x[k.place]).then_inc(e_stats, 1)

            def e_moments_of(k):
                after_apart(dve, (e_stats, k.n + 1))
                nc.vector.bn_aggr(e_mv[k.place % 2][:, :], e_st[:, :]).then_inc(e_moments, 1)

            def e_variance(k):
                var = e_mv[k.place % 2][:, 1:2]
                after(dve, e_moments, k.n + 1)
                nc.vector.tensor_scalar(var, var, EPS, None, ALU.add).then_inc(e_var, 1)

            def e_scale_of(k):
                p = k.place % 2
                after(dve, e_rstd, k.n + 1)
                nc.vector.tensor_tensor(e_rv[p][:, :], e_rs[p][:, :], val[:, bass.ds(k.n, 1)],
                                        ALU.mult).then_inc(e_scale, 1)

            def same_target(k):
                after(dve, sumT_ps, k.n - 1)
                after(dve, src_row_ld[k.place], 16 * (k.turn + 1))
                nc.vector.tensor_scalar(same[k.place % 2][:, :], src_row[k.place][:, :],
                                        src_f[:, bass.ds(k.n, 1)], None, ALU.is_equal).then_inc(same_rdy, 1)

            def e_norm(k):
                p = k.place % 2
                after(dve, e_scale, k.n + 1)
                after(dve, edge_lo_rdy, k.n)
                nc.vector.tensor_scalar(edge_xn, edge_x[k.place], e_mv[p][:, 0:1], e_rv[p][:, :],
                                        ALU.subtract, ALU.mult).then_inc(edge_xn_rdy, 1)

            def count_earlier(k):
                after(dve, same_rdy, k.n + 1)
                nc.vector.tensor_tensor_reduce(out=same_before[:, :], in0=f32(same[k.place % 2][:, :]),
                                               in1=before[:, :], scale=1.0, scalar=0.0, op0=ALU.mult,
                                               op1=ALU.add, accum_out=earlier[:, :]).then_inc(earlier_rdy, 1)

            def target_shift(k):
                after(dve, earlier_rdy, k.n + 1)
                nc.vector.tensor_scalar(shift[:, :], earlier[:, :], 1.0, to_spare[:, bass.ds(k.n, 1)],
                                        ALU.min, ALU.mult).then_inc(shift_rdy, 1)

            def target_of(k):
                after(dve, shift_rdy, k.n + 1)
                nc.vector.tensor_tensor(target[:, bass.ds(k.n, 1)], src_f[:, bass.ds(k.n, 1)], shift[:, :],
                                        ALU.add).then_inc(target_rdy, 1)

            def edge_low(k):
                low_part(edge_lo[:, :], edge_xn, edge_hi[:, :], edge_hi_rdy, k.n + 1, edge_lo_rdy)

            def sumT_low(k):
                hi, lo = sumT[k.place % 2]
                low_part(lo[:, :, :], chunked(p_sumT[k.place % 2]), hi[:, :, :], sumT_hi, k.n + 1, sumT_lo)

            def edges(k):
                k1, k2, k4 = k.plus(1), k.plus(2), k.plus(4)
                has2, has4 = k2.within(EDGE_TILES), k4.within(EDGE_TILES)
                if has2:
                    e_scale_of(k2)
                    same_target(k2)
                    e_norm(k2)
                    count_earlier(k2)
                if has4:
                    e_stats_of(k4)
                if k1.within(EDGE_TILES):
                    sumT_low(k1)
                if has2:
                    target_shift(k2)
                    edge_low(k2)
                if has4:
                    e_moments_of(k4)
                if has2:
                    target_of(k2)
                if has4:
                    e_variance(k4)

            for k in range(2):
                e_stats_of(four(k))
                e_moments_of(four(k))
                e_variance(four(k))
            gate_bias(pair(LEAD - 1))
            edges(four(-2))
            trans_bias(pair(LEAD - 1))
            for k in range(-1, EDGE_SLOTS):
                edges(four(k))
            a_moments_of(pair(LEAD))
            with dve.Fori(1, EDGE_TILES // EDGE_SLOTS - 1) as q:
                for place in range(EDGE_SLOTS):
                    edges(At(q, place, EDGE_SLOTS))
            for k in range(EDGE_TILES - EDGE_SLOTS, EDGE_TILES):
                edges(four(k))

            dve.wait_ge(a_var, LEAD + 1)
            a_moments_of(pair(LEAD + 1))
            xT_low(pair(LEAD))
            xT_low(pair(LEAD + 1))
            weight_lo(WW)
            weight_lo(WV)
            low_part(wg_parts[:, :, NE:], wg_raw[:, :, :], wg_parts[:, :, 0:NE], wg_hi, 1, wg_lo)

            def mix(u):
                after(dve, agg_ld[u.place], 16 * (u.turn + 1))
                trans = t_ring[:, u.n % LEAD, :]
                nc.vector.scalar_tensor_tensor(diff, agg_in[u.place], 0.0, trans, ALU.max,
                                               ALU.subtract).then_inc(diff_rdy, 1)
                after(dve, gate_tanh, u.n + 1)
                after(dve, diff_rdy, u.n + 1)
                nc.vector.scalar_tensor_tensor(diff, g_ring[:, u.n % LEAD, :], 1.0, diff, ALU.add,
                                               ALU.mult).then_inc(gated_rdy, 1)
                after(dve, gated_rdy, u.n + 1)
                nc.vector.scalar_tensor_tensor(mixed, diff, 0.5, trans, ALU.mult,
                                               ALU.add).then_inc(mixed_rdy, 1)

            def b_moments_of(u):
                after(dve, x1_rdy, u.n + 1)
                nc.vector.bn_stats(b_st[:, :], x_ring[:, u.n % X_RING, :]).then_inc(b_stats, 1)
                after_apart(dve, (b_stats, u.n + 1))
                nc.vector.bn_aggr(b_mv[:, :], b_st[:, :]).then_inc(b_moments, 1)

            def b_norm(u):
                after(dve, x1nT_ps, u.n)
                after(dve, b_rstd, u.n + 1)
                nc.vector.tensor_scalar(x1n, x_ring[:, u.n % X_RING, :], b_mv[:, 0:1], b_rs[:, :],
                                        ALU.subtract, ALU.mult).then_inc(x1n_rdy, 1)

            def x1nT_low(u):
                low_part(x1nT[1], chunked(p_x1nT), x1nT[0], x1nT_hi, u.n + 1, x1nT_lo)

            def hT_low(v):
                low_part(hT[1], chunked(p_hT), hT[0], hT_hi, v.n + 1, hT_lo)

            def activate(u):
                after(dve, h_rdy, u.n)
                after(dve, z_tanh_rdy, u.n + 1)
                nc.vector.scalar_tensor_tensor(act, z_tanh, 1.0, p_zw[:, :], ALU.add,
                                               ALU.mult).then_inc(silu_rdy, 1)

            def multiply(u):
                after(dve, zv_ps, u.n + 1)
                after(dve, silu_rdy, u.n + 1)
                nc.vector.tensor_tensor(act, act, p_zv[:, :], ALU.mult).then_inc(act_rdy, 1)

            def logits(u):
                after(dve, logit_ps, u.n + 1)
                nc.vector.tensor_copy(logit_parts[:, :], p_logit_rows).then_inc(logit_parts_rdy, 1)
                after(dve, logit_parts_rdy, u.n + 1)
                nc.vector.tensor_tensor(logit[:, :], logit_parts[:, 0:NE], logit_parts[:, NE:],
                                        ALU.add).then_inc(logit_rdy, 1)
                after_apart(dve, (logit_rdy, u.n + 1))
                nc.vector.max(best[:, :], logit[:, :]).then_inc(best_rdy, 1)
                after_apart(dve, (best_rdy, u.n + 1))
                nc.vector.max_index(best_i[:, :], best[:, :], logit[:, :]).then_inc(best_i_rdy, 1)
                nc.vector.tensor_tensor(gap[:, :], best[:, 1:2], best[:, 0:1], ALU.subtract).then_inc(gap_rdy, 1)
                after(dve, best_i_rdy, u.n + 1)
                nc.vector.tensor_copy(best_f[:, :], best_i[:, 0:2]).then_inc(best_f_rdy, 1)

            def shares(u):
                after(dve, e2_rdy, u.n + 1)
                nc.vector.tensor_scalar(total[:, :], e2[:, :], 1.0, 2.0, ALU.add, ALU.mult).then_inc(total_rdy, 1)
                after(dve, total_rdy, u.n + 1)
                nc.vector.reciprocal(share[:, 0:1], total[:, :]).then_inc(share1_rdy, 1)
                after(dve, share1_rdy, u.n + 1)
                nc.vector.tensor_tensor(share[:, 1:2], share[:, 0:1], e2[:, :], ALU.mult).then_inc(share2_rdy, 1)
                after(dve, best_f_rdy, u.n + 1)
                nc.vector.tensor_scalar(gw1[:, :], expert_f[:, :], best_f[:, 0:1], share[:, 0:1],
                                        ALU.is_equal, ALU.mult).then_inc(gw12_rdy, 1)
                after(dve, share2_rdy, u.n + 1)
                nc.vector.tensor_scalar(gw2[:, :], expert_f[:, :], best_f[:, 1:2], share[:, 1:2],
                                        ALU.is_equal, ALU.mult).then_inc(gw12_rdy, 1)
                after(dve, h_rdy, u.n)
                after(dve, gw12_rdy, 2 * u.n + 2)
                nc.vector.tensor_tensor(gw[:, :], gw1[:, :], gw2[:, :], ALU.add).then_inc(gw_rdy, 1)

            def residual(v):
                after(dve, out_st[v.place], 16 * v.turn)
                after(dve, y_ps, v.n + 1)
                nc.vector.tensor_tensor(out_sb[v.place], p_y[:, :], x_ring[:, v.n % X_RING, :],
                                        ALU.add).then_inc(out_rdy, 1)

            def rows(u):
                t = u.plus(LEAD)
                if not u.below(2):
                    xT_low(t)
                activate(u)
                multiply(u)
                logits(u)
                x1nT_low(u.plus(1))
                shares(u)
                if not u.below(1):
                    residual(u.plus(-1))
                mix(u.plus(2))
                if not u.below(2):
                    gate_bias(t)
                if t.plus(1).within(TILES) and not u.below(1):
                    a_moments_of(t.plus(1))
                b_moments_of(u.plus(2))
                if not u.below(2):
                    trans_bias(t)
                elif u.below(1):
                    trans_bias(t.plus(1))
                hT_low(u)
                b_norm(u.plus(2))

            def last_rows(u):
                if u.plus(2).within(TILES):
                    mix(u.plus(2))
                activate(u)
                logits(u)
                shares(u)
                multiply(u)
                if u.plus(1).within(TILES):
                    x1nT_low(u.plus(1))
                if u.plus(2).within(TILES):
                    b_moments_of(u.plus(2))
                residual(u.plus(-1))
                hT_low(u)
                if u.plus(2).within(TILES):
                    b_norm(u.plus(2))

            mix(pair(0))
            gate_bias(pair(LEAD))
            b_moments_of(pair(0))
            trans_bias(pair(LEAD))
            b_norm(pair(0))
            mix(pair(1))
            x1nT_low(pair(0))
            gate_bias(pair(LEAD + 1), p_y)
            b_moments_of(pair(1))
            b_norm(pair(1))
            weight_lo(WO)
            for u in range(4):
                rows(pair(u))
            with dve.Fori(2, (TILES - LEAD) // 2 - 1) as i:
                rows(At(i, 0, 2))
                rows(At(i, 1, 2))
            for u in range(TILES - LEAD - 2, TILES - LEAD):
                rows(pair(u))
            for u in range(TILES - LEAD, TILES):
                last_rows(pair(u))
            residual(pair(TILES - 1))

        @block.tensor
        def _(pe):
            def product(ps, lhsT, rhs):
                terms = [(lhsT[a], rhs[b], c) for c in range(C) for a, b in ((0, 0), (0, 1), (1, 0))]
                for n, (a, b, c) in enumerate(terms):
                    last = nc.tensor.matmul(ps, a[:, c, :], b[:, c, :], start=n == 0, stop=n == len(terms) - 1)
                return last

            def transposed(ps, rows):
                for c in range(C):
                    last = nc.tensor.transpose(ps[:, c * P:(c + 1) * P], rows[:, c * P:(c + 1) * P], ident[:, :])
                return last

            def gate_product(t, bank=None):
                if bank is None:
                    after(pe, gate_sb, t.n)
                    bank = p_gate
                after(pe, xT_lo, t.n + 1)
                product(bank[:, :], xT_parts[t.place], w3p).then_inc(gate_ps, 1)

            def trans_product(t):
                after(pe, trans_sb, t.n)
                product(p_trans[:, :], xT_parts[t.place], w2p).then_inc(trans_ps, 1)

            def column_means(i):
                pe.wait_ge(w_sum, i + 1)
                nc.tensor.matmul(p_mean[i][:, :], one_over_D, chunk_sum, start=True, stop=True).then_inc(w_mean, 1)

            pe.wait_ge(memset_done, 4)
            column_means(W3)
            column_means(W2)
            pe.wait_ge(w_lo, W3 + 1)

            def ahead(t):
                gate_product(t)
                trans_product(t)

            gate_product(pair(0))
            pe.wait_ge(w_lo, W2 + 1)
            trans_product(pair(0))
            ahead(pair(1))
            with pe.Fori(1, LEAD // 2) as i:
                ahead(At(i, 0, 2))
                ahead(At(i, 1, 2))
            ahead(pair(LEAD - 1))

            def sums(k):
                p = k.place % 2
                after(pe, edge_lo_rdy, k.n + 1)
                for c in range(C):
                    cols = slice(c * P, (c + 1) * P)
                    nc.tensor.matmul(p_sumT[p][:, cols], edge_hi[:, cols], same[p][:, :], start=True, stop=False)
                    last = nc.tensor.matmul(p_sumT[p][:, cols], edge_lo[:, cols], same[p][:, :],
                                            start=False, stop=True)
                last.then_inc(sumT_ps, 1)

            def messages(k):
                p = k.place % 2
                after(pe, msg_sb, k.n - 1)
                after(pe, sumT_lo, k.n + 1)
                product(p_msg[p][:, :], sumT[p], w1O).then_inc(msg_ps, 1)

            def edges(k):
                if k.plus(1).within(EDGE_TILES):
                    sums(k.plus(1))
                if k.within(EDGE_TILES):
                    messages(k)

            edges(four(-1))
            pe.wait_ge(w_lo, W1 + 1)
            for k in range(EDGE_SLOTS):
                edges(four(k))
            with pe.Fori(1, EDGE_TILES // EDGE_SLOTS - 1) as q:
                for place in range(EDGE_SLOTS):
                    edges(At(q, place, EDGE_SLOTS))
            for k in range(EDGE_TILES - EDGE_SLOTS, EDGE_TILES):
                edges(four(k))

            def x1n_transpose(u):
                after(pe, x1n_rdy, u.n + 1)
                transposed(p_x1nT, x1n).then_inc(x1nT_ps, 1)

            def logit_transpose(u):
                after_apart(pe, (logit_T_sb, u.n + 1))
                nc.tensor.transpose(p_logit_rows, logit_parts_T[:, :], ident[0:2 * NE, 0:2 * NE]).then_inc(logit_ps, 1)

            def experts_in(u):
                after(pe, x1nT_lo, u.n + 1)
                for c in range(C):
                    for part in range(2):
                        last = nc.tensor.matmul(p_logit_T, wg_parts[:, c, :], x1nT[part][:, c, :],
                                                start=c + part == 0, stop=c + part == C)
                last.then_inc(logit_T_ps, 1)
                product(p_zw[:, :], x1nT, wWp).then_inc(zw_ps, 1)
                if u.plus(LEAD).within(TILES):
                    product(p_zv[:, :], x1nT, wVp).then_inc(zv_ps, 1)
                    logit_transpose(u)
                else:
                    logit_transpose(u)
                    product(p_zv[:, :], x1nT, wVp).then_inc(zv_ps, 1)

            def h_transpose(u):
                after(pe, h_rdy, u.n + 1)
                transposed(p_hT, h).then_inc(hT_ps, 1)

            def experts_out(v):
                after(pe, out_rdy, v.n)
                if v.below(1):
                    pe.wait_ge(gate_sb, LEAD + 2)
                after(pe, hT_lo, v.n + 1)
                product(p_y[:, :], hT, w1O).then_inc(y_ps, 1)

            def rows(u):
                t = u.plus(LEAD)
                experts_in(u)
                if u.plus(1).within(TILES):
                    x1n_transpose(u.plus(1))
                if u.plus(-1).within(TILES):
                    experts_out(u.plus(-1))
                if u.below(1):
                    trans_product(t.plus(1))
                elif t.within(TILES) and not u.below(2):
                    gate_product(t)
                    trans_product(t)
                h_transpose(u)

            gate_product(pair(LEAD))
            trans_product(pair(LEAD))
            gate_product(pair(LEAD + 1), p_y)
            pe.wait_ge(ident_rdy, 1)
            x1n_transpose(pair(0))
            pe.wait_ge(wg_lo, 1)
            pe.wait_ge(w_lo, WV + 1)
            rows(pair(0))
            pe.wait_ge(w_lo, WO + 1)
            rows(pair(1))
            with pe.Fori(1, (TILES - LEAD) // 2 - 1) as i:
                rows(At(i, 0, 2))
                rows(At(i, 1, 2))
            for u in range(TILES - LEAD - 2, TILES):
                rows(pair(u))
            experts_out(pair(TILES - 1))


def kernel(x, src, dst, edge_weight, L0_gnn_w1, L0_gnn_w2, L0_gnn_w3, L0_gnn_b1, L0_gnn_b2, L0_gnn_b3,
           L0_ffn_Wg, L0_ffn_W, L0_ffn_V, L0_ffn_W2):
    import numpy as np
    import concourse.bacc as bacc
    from concourse.bass_utils import run_bass_kernel_spmd

    rows, d = x.shape
    padded = -(-rows // P) * P
    edge_rows = EDGE_SLOTS * P
    edges = -(-len(src) // edge_rows) * edge_rows
    if padded == rows:
        padded += P

    xp = np.zeros((padded, d), x.dtype)
    xp[:rows] = x
    srcp = np.full(edges, padded - 1, src.dtype)
    srcp[:len(src)] = src
    dstp = np.zeros(edges, dst.dtype)
    dstp[:len(dst)] = dst
    valp = np.zeros(edges, edge_weight.dtype)
    valp[:len(edge_weight)] = edge_weight

    def columns(a):
        return np.ascontiguousarray(np.asarray(a).reshape(-1, P).T)

    def transposed_tiles(a):
        a = a.reshape(-1, P, d // P, P)
        return np.ascontiguousarray(np.transpose(a, (0, 3, 2, 1))).reshape(padded, d)

    def experts_side_by_side(w):
        return np.ascontiguousarray(np.transpose(np.asarray(w), (1, 0, 2)).reshape(d, -1))

    arrays = {
        "x": xp, "xT": transposed_tiles(xp), "src_rows": srcp, "src_cols": columns(srcp), "dst_cols": columns(dstp),
        "val_cols": columns(valp), "w1": L0_gnn_w1, "w2": L0_gnn_w2, "w3": L0_gnn_w3,
        "b1": L0_gnn_b1, "b2": L0_gnn_b2, "b3": L0_gnn_b3, "wg": L0_ffn_Wg,
        "wW": experts_side_by_side(L0_ffn_W), "wV": experts_side_by_side(L0_ffn_V),
        "wO": np.asarray(L0_ffn_W2).reshape(-1, d),
    }
    arrays = {k: np.ascontiguousarray(v) for k, v in arrays.items()}
    nc = bacc.Bacc("TRN2", target_bir_lowering=False, num_devices=1)
    ins = {k: nc.dram_tensor("in_" + k, v.shape, mybir.dt.from_np(v.dtype), kind="ExternalInput").ap()
           for k, v in arrays.items()}
    out = nc.dram_tensor("out_rows", (padded, d), F32, kind="ExternalOutput").ap()
    gnn_experts_kernel(nc, **ins, out=out)
    r = run_bass_kernel_spmd(nc, [{"in_" + k: v for k, v in arrays.items()}], core_ids=[0])
    return r.results[0]["out_rows"][:rows]
```
